# Optimizing a Trainium2 kernel written in Bass

```python
import numpy as np
import jax
import jax.numpy as jnp

def _softmax(x, axis=-1):
    return jax.nn.softmax(x, axis=axis)

def _gelu(x):
    return jax.nn.gelu(x, approximate=True)

def _silu(x):
    return jax.nn.silu(x)

def _sigmoid(x):
    return jax.nn.sigmoid(x)

def _layernorm(x, axis=-1, eps=1e-05):
    m = jnp.mean(x, axis=axis, keepdims=True)
    v = jnp.var(x, axis=axis, keepdims=True)
    return (x - m) / jnp.sqrt(v + eps)

def _scatter_add(tgt, idx, src, axis=0):
    return tgt.at[idx].add(src)

def _segment_sum(src, seg, n):
    return jax.ops.segment_sum(src, seg, n)
kernel_name = 'mk_seq_postln_d2_jaxref_r4_d34d0b'

def setup_inputs(seed: int=0):
    np.random.seed(seed)
    _w = jnp.asarray

    def _L0_attn_setup():
        import jax, jax.numpy as jnp
        import numpy as np
        IN_FEATURES = 1024
        OUT_FEATURES = 1024
        WEIGHT_SPARSITY = 0.9
        key = jax.random.key(seed)
        kx, kw, km, kb = jax.random.split(key, 4)
        x = jax.random.normal(kx, (4, 512, IN_FEATURES), dtype=jnp.float32)
        dense_w = jax.random.normal(kw, (OUT_FEATURES, IN_FEATURES), dtype=jnp.float32)
        mask = jax.random.uniform(km, (OUT_FEATURES, IN_FEATURES)) >= WEIGHT_SPARSITY
        weight = dense_w * mask.astype(jnp.float32)
        bias = jax.random.uniform(kb, (OUT_FEATURES,), dtype=jnp.float32)
        return {'x': x, 'weight': weight, 'bias': bias}
    _L0_attn_in = _L0_attn_setup()

    def _L0_ffn_setup():
        import jax, jax.numpy as jnp
        import numpy as np
        RMS_EPS = 1e-05
        key = jax.random.key(seed)
        k1, k2, k3, k4 = jax.random.split(key, 4)
        B, S, H, I = (1, 512, 1024, 3584)
        x = jax.random.normal(k1, (B, S, H), dtype=jnp.float32)
        ln_w = jnp.ones((H,), dtype=jnp.float32)
        gate_w = jax.random.normal(k2, (I, H), dtype=jnp.float32) * 0.02
        up_w = jax.random.normal(k3, (I, H), dtype=jnp.float32) * 0.02
        down_w = jax.random.normal(k4, (H, I), dtype=jnp.float32) * 0.02
        return {'x': x, 'ln_w': ln_w, 'gate_w': gate_w, 'up_w': up_w, 'down_w': down_w}
    _L0_ffn_in = _L0_ffn_setup()

    def _L1_attn_setup():
        import jax, jax.numpy as jnp
        import numpy as np
        import math
        HIDDEN = 1024
        N_HEADS = 32
        N_KV_HEADS = 8
        HEAD_DIM = HIDDEN // N_HEADS
        GROUPS = N_HEADS // N_KV_HEADS
        ROPE_THETA = 10000.0
        TOKEN_BUDGET = 128
        INIT_BUDGET = 128
        RECENT_BUDGET = 128
        CHUNK = 16
        B, S = (1, 512)

        def _rotate_half(x):
            x1, x2 = jnp.split(x, 2, axis=-1)
            return jnp.concatenate([-x2, x1], axis=-1)

        def _rope(seq_len, dtype):
            inv_freq = 1.0 / ROPE_THETA ** (jnp.arange(0, HEAD_DIM, 2, dtype=jnp.float32) / HEAD_DIM)
            freqs = jnp.arange(seq_len, dtype=jnp.float32)[:, None] * inv_freq[None, :]
            emb = jnp.concatenate([freqs, freqs], axis=-1)
            return (jnp.cos(emb).astype(dtype), jnp.sin(emb).astype(dtype))
        key = jax.random.key(seed)
        ks = jax.random.split(key, 5)
        sc = 0.02
        return {'hidden_states': jax.random.normal(ks[0], (B, S, HIDDEN), dtype=jnp.float32), 'wq': jax.random.normal(ks[1], (N_HEADS * HEAD_DIM, HIDDEN), dtype=jnp.float32) * sc, 'wk': jax.random.normal(ks[2], (N_KV_HEADS * HEAD_DIM, HIDDEN), dtype=jnp.float32) * sc, 'wv': jax.random.normal(ks[3], (N_KV_HEADS * HEAD_DIM, HIDDEN), dtype=jnp.float32) * sc, 'wo': jax.random.normal(ks[4], (HIDDEN, N_HEADS * HEAD_DIM), dtype=jnp.float32) * sc}
    _L1_attn_in = _L1_attn_setup()

    def _L1_ffn_setup():
        import jax, jax.numpy as jnp
        import numpy as np
        NUM_EXPERTS = 8
        RANK = 32
        ALPHA = 16.0
        TOP_K = 2
        TEMPERATURE = 1.0
        GAMMA = 0.5
        SOFT_TOPK_TEMP = 0.5
        N_GRAM = 2
        EPS = 1e-06
        key = jax.random.key(seed)
        ks = jax.random.split(key, 6)
        d_in, d_out = (1024, 1024)
        Bsz, T = (4, 512)
        x = jax.random.normal(ks[0], (Bsz, T, d_in), dtype=jnp.float32)
        W = jax.random.normal(ks[1], (d_out, d_in), dtype=jnp.float32) / np.sqrt(d_in)
        b = jax.random.normal(ks[2], (d_out,), dtype=jnp.float32) * 0.01
        A = jax.random.normal(ks[3], (d_in, RANK), dtype=jnp.float32) / np.sqrt(d_in)
        Bmat = jax.random.normal(ks[4], (RANK, d_out), dtype=jnp.float32) * 0.01
        LiMEs = jax.random.normal(ks[5], (NUM_EXPERTS, RANK), dtype=jnp.float32) * 0.1
        return {'x': x, 'W': W, 'b': b, 'A': A, 'Bmat': Bmat, 'LiMEs': LiMEs}
    _L1_ffn_in = _L1_ffn_setup()
    _d = {'L0_attn_x': _L0_attn_in['x'], 'L0_attn_weight': _L0_attn_in['weight'], 'L0_attn_bias': _L0_attn_in['bias'], 'L0_ffn_ln_w': _L0_ffn_in['ln_w'], 'L0_ffn_gate_w': _L0_ffn_in['gate_w'], 'L0_ffn_up_w': _L0_ffn_in['up_w'], 'L0_ffn_down_w': _L0_ffn_in['down_w'], 'L1_attn_wq': _L1_attn_in['wq'], 'L1_attn_wk': _L1_attn_in['wk'], 'L1_attn_wv': _L1_attn_in['wv'], 'L1_attn_wo': _L1_attn_in['wo'], 'L1_ffn_W': _L1_ffn_in['W'], 'L1_ffn_b': _L1_ffn_in['b'], 'L1_ffn_A': _L1_ffn_in['A'], 'L1_ffn_Bmat': _L1_ffn_in['Bmat'], 'L1_ffn_LiMEs': _L1_ffn_in['LiMEs']}
    _x0 = _d['L0_attn_x']
    _d['L0_attn_x'] = jax.random.normal(jax.random.fold_in(jax.random.key(seed), 1), (4, 512, 1024), dtype=_x0.dtype)
    del _x0
    return _d

def reference(L0_attn_x, L0_attn_weight, L0_attn_bias, L0_ffn_ln_w, L0_ffn_gate_w, L0_ffn_up_w, L0_ffn_down_w, L1_attn_wq, L1_attn_wk, L1_attn_wv, L1_attn_wo, L1_ffn_W, L1_ffn_b, L1_ffn_A, L1_ffn_Bmat, L1_ffn_LiMEs):

    def _L0_attn_ref(x, weight, bias):
        import jax, jax.numpy as jnp
        import numpy as np
        IN_FEATURES = 1024
        OUT_FEATURES = 1024
        WEIGHT_SPARSITY = 0.9
        return jnp.einsum('bsi,oi->bso', x, weight) + bias

    def _L0_ffn_ref(x, ln_w, gate_w, up_w, down_w):
        import jax, jax.numpy as jnp
        import numpy as np
        RMS_EPS = 1e-05
        var = jnp.mean(jnp.square(x), axis=-1, keepdims=True)
        nx = x * jax.lax.rsqrt(var + RMS_EPS) * ln_w
        g = jnp.einsum('bsh,ih->bsi', nx, gate_w)
        u = jnp.einsum('bsh,ih->bsi', nx, up_w)
        return jnp.einsum('bsi,hi->bsh', jax.nn.silu(g) * u, down_w)

    def _L1_attn_ref(hidden_states, wq, wk, wv, wo):
        import jax, jax.numpy as jnp
        import numpy as np
        import math
        HIDDEN = 1024
        N_HEADS = 32
        N_KV_HEADS = 8
        HEAD_DIM = HIDDEN // N_HEADS
        GROUPS = N_HEADS // N_KV_HEADS
        ROPE_THETA = 10000.0
        TOKEN_BUDGET = 128
        INIT_BUDGET = 128
        RECENT_BUDGET = 128
        CHUNK = 16
        B, S = (1, 512)

        def _rotate_half(x):
            x1, x2 = jnp.split(x, 2, axis=-1)
            return jnp.concatenate([-x2, x1], axis=-1)

        def _rope(seq_len, dtype):
            inv_freq = 1.0 / ROPE_THETA ** (jnp.arange(0, HEAD_DIM, 2, dtype=jnp.float32) / HEAD_DIM)
            freqs = jnp.arange(seq_len, dtype=jnp.float32)[:, None] * inv_freq[None, :]
            emb = jnp.concatenate([freqs, freqs], axis=-1)
            return (jnp.cos(emb).astype(dtype), jnp.sin(emb).astype(dtype))
        b, s, _ = hidden_states.shape
        dtype = hidden_states.dtype
        NEG = jnp.finfo(dtype).min
        q = (hidden_states @ wq.T).reshape(b, s, N_HEADS, HEAD_DIM).transpose(0, 2, 1, 3)
        k = (hidden_states @ wk.T).reshape(b, s, N_KV_HEADS, HEAD_DIM).transpose(0, 2, 1, 3)
        v = (hidden_states @ wv.T).reshape(b, s, N_KV_HEADS, HEAD_DIM).transpose(0, 2, 1, 3)
        cos, sin = _rope(s, dtype)
        q = q * cos[None, None] + _rotate_half(q) * sin[None, None]
        k = k * cos[None, None] + _rotate_half(k) * sin[None, None]
        k = jnp.repeat(k, GROUPS, axis=1)
        v = jnp.repeat(v, GROUPS, axis=1)
        scores = jnp.einsum('bhqd,bhkd->bhqk', q, k) / math.sqrt(HEAD_DIM)
        q_pos = jnp.arange(s)[:, None]
        k_pos = jnp.arange(s)[None, :]
        causal = k_pos <= q_pos
        masked = jnp.where(causal[None, None], scores, NEG)
        pad = -s % CHUNK
        padded = jnp.pad(masked, ((0, 0), (0, 0), (0, 0), (0, pad)), constant_values=NEG)
        n_chunks = (s + pad) // CHUNK
        chunk_max = padded.reshape(b, N_HEADS, s, n_chunks, CHUNK).max(axis=-1)
        k_top = min(max(3, TOKEN_BUDGET // CHUNK), n_chunks)
        _, topk_idx = jax.lax.top_k(chunk_max, k_top)
        chunk_mask = jnp.any(topk_idx[..., None] == jnp.arange(n_chunks), axis=-2)
        tok_mask = jnp.repeat(chunk_mask, CHUNK, axis=-1)[..., :s]
        init_mask = k_pos < INIT_BUDGET
        recent_mask = k_pos > q_pos - RECENT_BUDGET
        allowed = causal[None, None] & (tok_mask | init_mask[None, None] | recent_mask[None, None])
        final = jnp.where(allowed, scores, NEG)
        attn = jax.nn.softmax(final, axis=-1)
        out = jnp.einsum('bhqk,bhkd->bhqd', attn, v)
        out = out.transpose(0, 2, 1, 3).reshape(b, s, N_HEADS * HEAD_DIM)
        return out @ wo.T

    def _L1_ffn_ref(x, W, b, A, Bmat, LiMEs):
        import jax, jax.numpy as jnp
        import numpy as np
        NUM_EXPERTS = 8
        RANK = 32
        ALPHA = 16.0
        TOP_K = 2
        TEMPERATURE = 1.0
        GAMMA = 0.5
        SOFT_TOPK_TEMP = 0.5
        N_GRAM = 2
        EPS = 1e-06
        Bsz, T, d_in = x.shape
        E = LiMEs.shape[0]
        scaling = ALPHA / RANK
        H = jnp.einsum('btd,od->bto', x, W) + b
        z = jnp.einsum('btd,dr->btr', x, A)
        anchors = jnp.arange(N_GRAM - 1, T, N_GRAM)
        H_slice = H[:, anchors, :E]
        delta_slice = jnp.einsum('bar,er->bae', z[:, anchors], LiMEs)
        H_scale = jnp.maximum(jnp.max(jnp.abs(H_slice)), EPS)
        d_scale = jnp.maximum(jnp.max(jnp.abs(delta_slice)), EPS)
        logits = ((1.0 - GAMMA) * (H_slice / H_scale) + GAMMA * (delta_slice / d_scale)) / TEMPERATURE
        probs = jax.nn.softmax(logits, axis=-1)
        topk_vals, _ = jax.lax.top_k(probs, TOP_K)
        thresh = topk_vals[..., -1:]
        mask = jax.nn.sigmoid((probs - thresh) / SOFT_TOPK_TEMP)
        weights = probs * mask
        weights = weights / (jnp.sum(weights, axis=-1, keepdims=True) + 1e-09)
        weights_full = jnp.repeat(weights, N_GRAM, axis=1)
        p_mix = jnp.einsum('bte,er->btr', weights_full, LiMEs)
        delta = jnp.einsum('btr,ro->bto', z * p_mix, Bmat) * scaling
        return H + delta
    x = L0_attn_x
    x = _layernorm(x + _L0_attn_ref(x, L0_attn_weight, L0_attn_bias), axis=-1)
    x = _layernorm(x + _L0_ffn_ref(x, L0_ffn_ln_w, L0_ffn_gate_w, L0_ffn_up_w, L0_ffn_down_w), axis=-1)
    x = _layernorm(x + _L1_attn_ref(x, L1_attn_wq, L1_attn_wk, L1_attn_wv, L1_attn_wo), axis=-1)
    x = _layernorm(x + _L1_ffn_ref(x, L1_ffn_W, L1_ffn_b, L1_ffn_A, L1_ffn_Bmat, L1_ffn_LiMEs), axis=-1)
    return x

_drawn_inputs = setup_inputs


def setup_inputs(seed=0):
    import zlib

    import numpy as np

    out = dict(_drawn_inputs(seed))
    spreads = {'L0_ffn_ln_w': (1.0, 0.2)}
    factors = {'L1_attn_wq': 3.063,
     'L1_attn_wk': 3.041,
     'L1_ffn_b': 8.0,
     'L1_ffn_A': 8.0,
     'L1_ffn_Bmat': 8.0,
     'L1_ffn_LiMEs': 8.0}
    for name, (base, spread) in spreads.items():
        noise = np.random.default_rng([zlib.crc32(name.encode()), seed]).standard_normal(out[name].shape)
        drawn = base * np.exp(spread * noise) if base else spread * noise
        out[name] = jnp.asarray(drawn.astype(out[name].dtype))
    for name, factor in factors.items():
        out[name] = (out[name] * factor).astype(out[name].dtype)
    return out
```

```python
from contextlib import ExitStack

import numpy as np

import concourse.bass as bass
from concourse import mybir

P = 128
NB = 4
T = 512
D = 1024
KC = D // P
FF = 3584
G = 4
NG = FF // P // G
NH, NKV, HD = 32, 8, 32
QT = T // P
CHUNK, TOPK = 16, 8
NE, RANK = 8, 32
LN_EPS = 1e-5
SCALE = float(HD) ** -0.5
NEG = -1e38
MARK = 3e38

A_N, B_N, C_N, E_N, F_N = KC, NG * (2 * G + 4), 20, 1, KC
A_W = 0
B_W = A_W + A_N
C_W = B_W + B_N
E_W = C_W + C_N
F_W = E_W + E_N
N_UNITS = F_W + F_N
A_U = 0
B_U = A_U + NB * A_N
C_U = B_U + NB * B_N
E_U = C_U + NB * C_N
F_U = E_U + NB * E_N
RING = 4
B_FREED = NG * KC
B_FV = NB * KC
C_FV = B_FV + NB * B_FREED
F_FV = C_FV + NB * KC
C_FA = 12
EW = RANK + NE
MAXED, SHIFTED, ABOVE, WEIGHED, TURNED_W, MIXED = 4, 11, 23, 30, 32, 34
V_POS = [0, 128, 224, 352]
V_WIN = [V_POS[r] - HD * r for r in range(4)]
V_ROW = 384

ALU = mybir.AluOpType
ACT = mybir.ActivationFunctionType
AX = mybir.AxisListType.X
F32 = mybir.dt.float32
F32R = mybir.dt.float32r
BF16 = mybir.dt.bfloat16
RMAX = bass.bass_isa.ReduceOp.max


def build(nc, io):
    with ExitStack() as ctx:
        def sb(name, shape, dt=F32):
            return ctx.enter_context(nc.sbuf_tensor(name, shape, dt))

        def sem(name):
            return ctx.enter_context(nc.semaphore(name))

        x = sb("x", [P, NB, KC, T])
        xs_h = sb("xs_h", [P, KC, T], F32R)
        xs_l = sb("xs_l", [P, KC, T], F32R)
        raw = sb("raw", [P, 2, KC * P])
        w_h = sb("w_h", [P, RING, KC * P], F32R)
        w_l = sb("w_l", [P, RING, KC * P], F32R)
        full_sum = sb("full_sum", [P, T])
        ones = sb("ones", [P, P])
        ident = sb("ident", [P, P])
        ident_b = sb("ident_b", [P, P], BF16)
        causal_b = sb("causal_b", [P, P], BF16)
        old = sb("old", [P, 2 * P])
        bias0 = sb("bias0", [P, KC])
        lnw = sb("lnw", [P, KC])
        bias1 = sb("bias1", [P, KC])
        bias_e = sb("bias_e", [P, 1])
        eps = sb("eps", [P, 1])

        def place(*tensors):
            with ExitStack() as own:
                return [own.enter_context(nc.sbuf_tensor(n, s, d)) for n, s, d in tensors]

        sq, sq_sum, sd, rstd, part_sum = place(
            ("sq", [P, 2, T], F32), ("sq_sum", [P, T], F32), ("sd", [P, T], F32), ("rstd", [P, T], F32),
            ("part_sum", [P, T], F32))
        prob, pt_h, pt_l = place(("prob", [P, 2, T], F32), ("pt_h", [P, 2, T], F32R), ("pt_l", [P, 2, T], F32R))
        sb("norm_or_attention", [P, 6 * T])
        hs_h, hs_l, h_raw, silu_g, var_x, nx, r_rms = place(
            ("hs_h", [P, 2, G, T], F32R), ("hs_l", [P, 2, G, T], F32R), ("h_raw", [P, 2, T], F32),
            ("silu_g", [P, 2, T], F32), ("var_x", [P, NB, T], F32), ("nx", [P, 2, T], F32),
            ("r_rms", [P, T], F32))
        vp_h, vp_l, kt_h, kt_l, qf, v_f, qs_h, qs_l, rope_a, rope_b, cos_t, sin_t, small = place(
            ("vp_h", [P, QT, V_ROW], F32R), ("vp_l", [P, QT, V_ROW], F32R),
            ("kt_h", [P, 2, T], F32R), ("kt_l", [P, 2, T], F32R), ("qf", [P, KC, T], F32),
            ("v_f", [P, QT, 2 * P], F32), ("qs_h", [P, T], F32R), ("qs_l", [P, T], F32R),
            ("rope_a", [P, T], F32), ("rope_b", [P, T], F32), ("cos_t", [P, T], F32),
            ("sin_t", [P, T], F32), ("small", [P, 768], F32))
        zh, zp, zs_h, zs_l, b_raw, bm_h, bm_l, li, li_t, rt = place(
            ("zh", [P, NB * T], F32), ("zp", [RANK, NB * T], F32), ("zs_h", [RANK, T], F32R),
            ("zs_l", [RANK, T], F32R), ("b_raw", [RANK, D], F32), ("bm_h", [RANK, D], F32R),
            ("bm_l", [RANK, D], F32R), ("li", [NE, RANK], F32), ("li_t", [RANK, NE], F32),
            ("rt", [P, 1024 + NB * T // 2], F32))

        def two(at, n):
            return [small[:, at:at + n], small[:, at + n:at + 2 * n]]

        cmaxs, top8s, marks, pens_c = two(0, 32), two(64, 8), two(80, 32), two(144, 32)
        pen, rinvs = small[:, 208:464], two(464, P)
        nbias, rsum, rmax = small[:, 720:736], small[:, 736:752], small[:, 752:768]

        banks = ctx.enter_context(nc.psum_tensor("banks", [P, 8, 512], F32))
        ln_bank, o_bank = banks[:, 4, :], banks[:, 6, :]
        t_bank = [banks[:, 5, :], banks[:, 7, :]]

        x0_in = [sem(f"x0_in{k}") for k in range(KC)]
        x_in = sem("x_in")
        consts_in = sem("consts_in")
        rope_in = sem("rope_in")
        late_in = sem("late_in")
        raw_in = [sem(f"raw_in{i}") for i in range(2)]
        unit_hi = sem("unit_hi")
        unit_lo = sem("unit_lo")
        unit_done = sem("unit_done")
        xs_hi = sem("xs_hi")
        xs_lo = sem("xs_lo")
        xs_free = sem("xs_free")
        freed_v = sem("freed_v")
        freed_a = sem("freed_a")
        summed = sem("summed")
        mean_ok = sem("mean_ok")
        centred = sem("centred")
        squared = sem("squared")
        sq_added = sem("sq_added")
        var_ok = sem("var_ok")
        sd_ok = sem("sd_ok")
        rstd_ok = sem("rstd_ok")
        normed = sem("normed")
        ms_half = sem("ms_half")
        ms_ok = sem("ms_ok")
        rms_root = sem("rms_root")
        rms_ok = sem("rms_ok")
        nx_ok = sem("nx_ok")
        silu_ok = sem("silu_ok")
        h_ok = sem("h_ok")
        h_hi = sem("h_hi")
        h_lo = sem("h_lo")
        rope_st = sem("rope_st")
        roped = sem("roped")
        roped_hi = sem("roped_hi")
        roped_lo = sem("roped_lo")
        vp_zero = sem("vp_zero")
        vp_hi = sem("vp_hi")
        vp_lo = sem("vp_lo")
        scored = sem("scored")
        sel = sem("sel")
        nb_ok = sem("nb_ok")
        p_ok = sem("p_ok")
        turned = sem("turned")
        pt_hi = sem("pt_hi")
        pt_lo = sem("pt_lo")
        pv_ok = sem("pv_ok")
        rinv_ok = sem("rinv_ok")
        rinv_t = sem("rinv_t")
        o_ok = sem("o_ok")
        r_copied = sem("r_copied")
        z_ok = sem("z_ok")
        rtp = sem("rtp")
        rtv = sem("rtv")
        rta = sem("rta")
        rtg = sem("rtg")
        bm_hi = sem("bm_hi")
        bm_lo = sem("bm_lo")
        zs_hi = sem("zs_hi")
        zs_lo = sem("zs_lo")
        out_done = sem("out_done")
        block = ctx.enter_context(nc.Block())


        @block.sync
        def _(sp):
            def load(u, slot, src):
                sp.dma_start(raw[:, slot, :], io["units"][src]).then_inc(raw_in[slot], 16)

            def pair(u, src):
                for s in range(2):
                    sp.wait_ge(unit_lo, u + s - 1)
                    load(u + s, s, src + s)

            load(0, 0, A_W)
            load(1, 1, A_W + 1)
            for n in range(2, A_N, 2):
                pair(n, A_W + n)
            with sp.Fori(1, NB) as b:
                with sp.Fori(0, A_N // 2) as n:
                    pair(A_U + b * A_N + n * 2, A_W + n * 2)
            for base, count, src in ((B_U, B_N, B_W), (C_U, C_N, C_W)):
                with sp.Fori(0, NB) as b:
                    with sp.Fori(0, count // 2) as n:
                        pair(base + b * count + n * 2, src + n * 2)
            for b in range(NB):
                sp.wait_ge(unit_lo, E_U + b - 1)
                load(E_U + b, b % 2, E_W)
            with sp.Fori(0, NB) as b:
                with sp.Fori(0, F_N // 2) as n:
                    pair(F_U + b * F_N + n * 2, F_W + n * 2)
            with sp.Fori(0, NB) as b:
                sp.wait_ge(normed, (12 + b + 1) * KC)
                sp.dma_start(io["out"][b], x[:, b, :, :]).then_inc(out_done, 16)
            sp.wait_ge(out_done, 16 * NB)

        @block.gpsimd
        def _(pool):
            pool.wait_ge(rtv, MAXED)
            nc.gpsimd.partition_all_reduce(rt[:, 130:132], rt[:, 128:130], P, RMAX).then_inc(rtg, 1)

        @block.scalar
        def _(act):
            for k in range(KC):
                act.dma_start(x[:, 0, k, :], io["x"][0, :, k, :]).then_inc(x0_in[k], 16)
            for dst, name in ((ones, "ones"), (ident, "ident"), (ident_b, "ident_b"), (causal_b, "causal_b"),
                              (old, "old"), (bias0, "bias0"), (lnw, "lnw"), (bias1, "bias1"),
                              (bias_e, "bias_e"), (eps, "eps")):
                act.dma_start(dst[:], io[name]).then_inc(consts_in, 16)
            for b in range(1, NB):
                act.dma_start(x[:, b, :, :], io["x"][b]).then_inc(x_in, 16)
            copy = ACT.Copy

            def split_unit(u, n):
                act.wait_ge(raw_in[n % 2], 8 * (u - n % 2) + 16)
                if not isinstance(u, int) or u >= RING:
                    act.wait_ge(unit_done, u - RING + 1)
                nc.scalar.activation(w_h[:, n % RING, :], raw[:, n % 2, :], copy).then_inc(unit_hi, 1)

            def post(u):
                act.wait_ge(unit_done, u + 1)

            def ln_squares(n, p):
                for k in range(KC):
                    act.wait_ge(centred, n * KC + k + 1)
                    if k >= 2:
                        act.wait_ge(sq_added, n * 7 + max(1, k - 2))
                    nc.scalar.activation(sq[:, k % 2, :], x[:, p, k, :], ACT.Square).then_inc(squared, 1)

            def ln_root(n):
                act.wait_ge(var_ok, n + 1)
                nc.scalar.activation(sd[:], ln_bank, ACT.Sqrt, bias=eps[:]).then_inc(sd_ok, 1)

            def chunk_free(b, k):
                if k < KC - 1:
                    act.wait_ge(xs_free, b * (KC - 1) + k + 1)
                else:
                    act.wait_ge(unit_done, A_U + (b + 1) * A_N)

            def fill(b, ready):
                for k in range(KC):
                    ready(k)
                    nc.scalar.activation(xs_h[:, k, :], x[:, b, k, :], copy).then_inc(xs_hi, 1)

            for n in range(RING):
                split_unit(n, n)
                if n == 0:
                    fill(0, lambda k: act.wait_ge(x0_in[k], 16))
            act.wait_ge(consts_in, 160)

            def a_block(b, ln, more):
                for n in range(A_N):
                    if n == A_N - 1 and more:
                        act.wait_ge(x_in, 16 * (NB - 1))
                        fill(b + 1, lambda k: chunk_free(b, k))
                    elif n == A_N - 1:
                        rms_fill(0, free=lambda k: chunk_free(NB - 1, k))
                    post(A_U + b * A_N + n)
                    split_unit(A_U + b * A_N + n + RING, n)
                    if ln and n == 1:
                        ln_squares(b - 1, b - 1)
                    if ln and n == 5:
                        ln_root(b - 1)

            def rms_fill(b, free=lambda k: None):
                act.wait_ge(ms_ok, b + 1)
                nc.scalar.activation(r_rms[:], var_x[:, b, :], ACT.Sqrt, bias=eps[:]).then_inc(rms_root, 1)
                for k in range(KC):
                    free(k)
                    act.wait_ge(nx_ok, b * KC + k + 1)
                    nc.scalar.activation(xs_h[:, k, :], nx[:, k % 2, :], copy, scale=lnw[:, k:k + 1]).then_inc(xs_hi, 1)

            a_block(0, False, True)
            with act.Fori(1, NB - 1) as b:
                a_block(b, True, True)
            a_block(NB - 1, True, False)

            def gate_up(u0, h0, buf, norm_of=None):
                for i in range(G):
                    post(u0 + 2 * i)
                    if i >= 2 or norm_of is None:
                        act.wait_ge(h_ok, h0 + i - 1)
                    nc.scalar.activation(silu_g[:, i % 2, :], banks[:, 2 * i % RING, :], ACT.Silu).then_inc(silu_ok, 1)
                    split_unit(u0 + 2 * i + RING, 2 * i)
                    act.wait_ge(h_ok, h0 + i + 1)
                    nc.scalar.activation(hs_h[:, buf, i, :], h_raw[:, i % 2, :], copy).then_inc(h_hi, 1)
                    post(u0 + 2 * i + 1)
                    split_unit(u0 + 2 * i + 1 + RING, 2 * i + 1)
                    if norm_of is not None and i == 0:
                        ln_squares(*norm_of)
                    if norm_of is not None and i == 2:
                        ln_root(norm_of[0])

            def down(u0):
                for q in range(4):
                    post(u0 + q)
                    split_unit(u0 + q + RING, q)

            def b_block(b, more):
                ub, hb = B_U + b * B_N, b * NG * G
                gate_up(ub, hb, 0, norm_of=(3 + b, (b + 3) % NB))
                with act.Fori(0, NG // 2) as j:
                    gate_up(ub + 8 + j * 24, hb + 4 + j * 8, 1)
                    down(ub + 16 + j * 24)
                    gate_up(ub + 20 + j * 24, hb + 8 + j * 8, 0)
                    down(ub + 28 + j * 24)
                if more:
                    rms_fill(b + 1)
                down(ub + 80)

            with act.Fori(0, NB - 1) as b:
                b_block(b, True)
            b_block(NB - 1, False)

            act.dma_start(cos_t[:], io["cos"]).then_inc(rope_in, 16)
            act.dma_start(sin_t[:], io["sin"]).then_inc(rope_in, 16)
            act.wait_ge(vp_zero, 2)
            with act.Fori(0, NB) as b:
                fill(b, lambda k: act.wait_ge(normed, (4 + b) * KC + k + 1))
                uc = C_U + b * C_N
                for n in range(12):
                    post(uc + n)
                    if n in (2, 3):
                        v_dst = v_f[:, 2 * (n - 2):2 * (n - 2) + 2, :].rearrange("p t c -> p (t c)")
                        nc.scalar.activation(v_dst, banks[:, n, :], copy).then_inc(freed_a, 1)
                    else:
                        if n in (4, 5):
                            act.wait_ge(roped, 10 * b + n - 3)
                        nc.scalar.activation(qf[:, n if n < 2 else n - 4, :], banks[:, n % RING, :], copy)\
                            .then_inc(freed_a, 1)
                    split_unit(uc + n + RING, n)
                    if n in (1, 2):
                        act.wait_ge(roped, 10 * b + n)
                        nc.scalar.activation(kt_h[:, n - 1, :], rope_b[:], copy).then_inc(roped_hi, 1)
                    if n == 5:
                        ln_squares(7 + b, (b + 3) % NB)
                    if n == 9:
                        ln_root(7 + b)
                for half in range(2):
                    for r in range(4):
                        nc.scalar.activation(vp_h[:, :, V_POS[r]:V_POS[r] + HD],
                                             v_f[:, :, half * P + r * HD:half * P + r * HD + HD], copy)\
                            .then_inc(vp_hi, 1)
                    with act.Fori(0, 4) as j:
                        a = 8 * b + 4 * half + j
                        act.wait_ge(roped, 10 * b + 3 + 4 * half + j)
                        nc.scalar.activation(qs_h[:], rope_b[:], copy).then_inc(roped_hi, 1)

                        def turned_hi(i):
                            n = P * (i // 4 + 1)
                            act.wait_ge(turned, 16 * a + i + 1)
                            if i >= 2:
                                act.wait_ge(pv_ok, 16 * a + i - 1)
                            nc.scalar.activation(pt_h[:, i % 2, 0:n], t_bank[i % 2][:, 0:n], copy).then_inc(pt_hi, 1)

                        for i in range(16):
                            n = P * (i // 4 + 1)
                            act.wait_ge(nb_ok, 16 * a + i + 1)
                            if i >= 2:
                                act.wait_ge(turned, 16 * a + i - 1)
                            nc.scalar.activation(prob[:, i % 2, 0:n], banks[:, i % 4, 0:n], ACT.Exp,
                                                 bias=nbias[:, i:i + 1], scale=SCALE,
                                                 accum_out=rsum[:, i:i + 1]).then_inc(p_ok, 1)
                            if i >= 1:
                                turned_hi(i - 1)
                        turned_hi(15)
                        act.wait_ge(rinv_t, 4 * a + 4)
                        nc.scalar.activation(rope_a[:], ln_bank, copy).then_inc(r_copied, 1)
                        act.wait_ge(o_ok, a + 1)
                        nc.scalar.activation(xs_h[:, 4 * half + j, :], rope_b[:], copy).then_inc(xs_hi, 1)
                for n in range(12, 20):
                    post(uc + n)
                    split_unit(uc + n + RING, n)

            act.dma_start(b_raw[:], io["bmat"]).then_inc(late_in, 16)
            act.dma_start(li[:], io["li"]).then_inc(late_in, 16)
            act.dma_start(li_t[:], io["li_t"]).then_inc(late_in, 16)
            for b in range(NB):
                fill(b, lambda k: act.wait_ge(normed, (8 + b) * KC + k + 1))
                post(E_U + b)
                nc.scalar.activation(zh[0:EW, b * T:(b + 1) * T], banks[0:EW, b, :], ACT.Identity,
                                     bias=bias_e[0:EW, :]).then_inc(freed_a, 1)
                split_unit(E_U + b + RING, b)
                if b == 0:
                    ln_squares(11, NB - 1)
                if b == 1:
                    ln_root(11)
            act.wait_ge(late_in, 48)
            nc.scalar.activation(bm_h[:], b_raw[:], copy).then_inc(bm_hi, 1)
            act.wait_ge(rtv, SHIFTED)
            nc.scalar.activation(rt[:, 320:384], rt[:, 256:320], ACT.Exp).then_inc(rta, 1)
            act.wait_ge(rtv, ABOVE)
            nc.scalar.activation(rt[:, 640:704], rt[:, 576:640], ACT.Exp, scale=-2.0).then_inc(rta, 1)
            act.wait_ge(rtv, MIXED)

            def f_block(b, ln, more):
                fill(b, lambda k: None)
                nc.scalar.activation(zs_h[:], zp[:, bass.ds(b * T, T)], copy).then_inc(zs_hi, 1)
                for n in range(F_N):
                    post(F_U + b * F_N + n)
                    if more or n < 4:
                        split_unit(F_U + b * F_N + n + RING, n)
                    if ln and n == 1:
                        ln_squares(11 + b, b - 1)
                    if ln and n == 5:
                        ln_root(11 + b)
            f_block(0, False, True)
            with act.Fori(1, NB - 1) as b:
                f_block(b, True, True)
            f_block(NB - 1, True, False)
            ln_squares(15, NB - 1)
            ln_root(15)

        @block.vector
        def _(dve):
            tt = nc.vector.tensor_tensor
            ts = nc.vector.tensor_scalar
            stt = nc.vector.scalar_tensor_tensor
            sub, add, mul = ALU.subtract, ALU.add, ALU.mult

            def split_unit(u, n):
                dve.wait_ge(unit_hi, u + 1)
                tt(w_l[:, n % RING, :], raw[:, n % 2, :], w_h[:, n % RING, :].bitcast(F32), sub).then_inc(unit_lo, 1)

            def fill(f, b):
                for k in range(KC):
                    dve.wait_ge(xs_hi, f * KC + k + 1)
                    tt(xs_l[:, k, :], x[:, b, k, :], xs_h[:, k, :].bitcast(F32), sub).then_inc(xs_lo, 1)

            def rms_fill(b):
                dve.wait_ge(rms_root, b + 1)
                nc.vector.reciprocal(r_rms[:], r_rms[:]).then_inc(rms_ok, 1)
                dve.wait_ge(rms_ok, b + 1)

                def lo(k):
                    dve.wait_ge(xs_hi, (4 + b) * KC + k + 1)
                    stt(xs_l[:, k, :], nx[:, k % 2, :], lnw[:, k:k + 1], xs_h[:, k, :].bitcast(F32), mul, sub)\
                        .then_inc(xs_lo, 1)
                for k in range(KC):
                    if k >= 2:
                        dve.wait_ge(xs_lo, (4 + b) * KC + k - 1)
                    tt(nx[:, k % 2, :], x[:, b, k, :], r_rms[:], mul).then_inc(nx_ok, 1)
                    if k >= 1:
                        lo(k - 1)
                lo(KC - 1)

            def post(u):
                dve.wait_ge(unit_done, u + 1)

            def add_chunk(n, b, o, freed):
                if o == 0:
                    return
                dve.wait_ge(freed_v, freed)
                if o >= 2:
                    dve.wait_ge(summed, n * 7 + o - 1)
                dst = full_sum if o == KC - 1 else part_sum
                tt(dst[:], x[:, b, o, :], x[:, b, 0, :] if o == 1 else part_sum[:], add).then_inc(summed, 1)

            def ln_centre(n, p):
                dve.wait_ge(mean_ok, n + 1)
                for k in range(KC):
                    tt(x[:, p, k, :], x[:, p, k, :], ln_bank, sub).then_inc(centred, 1)
                for k in range(1, KC):
                    dve.wait_ge(squared, n * KC + k + 1)
                    if k >= 2:
                        dve.wait_ge(sq_added, n * 7 + k - 1)
                    tt(sq_sum[:], sq[:, k % 2, :], sq[:, 0, :] if k == 1 else sq_sum[:], add).then_inc(sq_added, 1)

            def ln_scale(n, p, keep=False):
                dve.wait_ge(sd_ok, n + 1)
                nc.vector.reciprocal(rstd[:], sd[:]).then_inc(rstd_ok, 1)
                dve.wait_ge(rstd_ok, n + 1)
                if keep:
                    tt(var_x[:, p, :], rstd[:], ln_bank, mul).then_inc(ms_half, 1)
                for k in range(KC):
                    tt(x[:, p, k, :], x[:, p, k, :], rstd[:], mul).then_inc(normed, 1)
                if keep:
                    dve.wait_ge(ms_half, n + 1)
                    tt(var_x[:, p, :], var_x[:, p, :], rstd[:], mul).then_inc(ms_ok, 1)

            for n in range(RING):
                split_unit(n, n)
                if n == 0:
                    fill(0, 0)
            dve.wait_ge(consts_in, 160)

            def a_block(b, ln, more):
                for n in range(A_N):
                    if n == A_N - 1:
                        fill(b + 1, b + 1) if more else rms_fill(0)
                    post(A_U + b * A_N + n)
                    xo = x[:, b, n, :]
                    stt(xo, banks[:, n % RING, :], bias0[:, n:n + 1], xo, add, add).then_inc(freed_v, 1)
                    split_unit(A_U + b * A_N + n + RING, n)
                    add_chunk(b, b, n, b * KC + n + 1)
                    if ln and n == 1:
                        ln_centre(b - 1, b - 1)
                    if ln and n == 5:
                        ln_scale(b - 1, b - 1, keep=True)

            a_block(0, False, True)
            with dve.Fori(1, NB - 1) as b:
                a_block(b, True, True)
            a_block(NB - 1, True, False)

            def gate_up(u0, h0, buf, norm_of=None):
                def lo(i):
                    dve.wait_ge(h_hi, h0 + i + 1)
                    tt(hs_l[:, buf, i, :], h_raw[:, i % 2, :], hs_h[:, buf, i, :].bitcast(F32), sub).then_inc(h_lo, 1)
                for i in range(G):
                    post(u0 + 2 * i)
                    split_unit(u0 + 2 * i + RING, 2 * i)
                    post(u0 + 2 * i + 1)
                    dve.wait_ge(silu_ok, h0 + i + 1)
                    tt(h_raw[:, i % 2, :], banks[:, (2 * i + 1) % RING, :], silu_g[:, i % 2, :], mul).then_inc(h_ok, 1)

                    split_unit(u0 + 2 * i + 1 + RING, 2 * i + 1)
                    lo(i)
                    if norm_of is not None and i == 0:
                        ln_centre(*norm_of)
                    if norm_of is not None and i == 2:
                        ln_scale(*norm_of, keep=True)

            def down(b, u0, last=False):
                for q in range(4):
                    post(u0 + q)
                    for o in (2 * q, 2 * q + 1):
                        xo = x[:, b, o, :]
                        tt(xo, banks[:, o % RING, :], xo, add).then_inc(freed_v, 1)
                    split_unit(u0 + q + RING, q)
                    if last:
                        for o in (2 * q, 2 * q + 1):
                            add_chunk(4 + b, b, o, B_FV + (b + 1) * B_FREED - KC + o + 1)

            def b_block(b, more):
                ub, hb = B_U + b * B_N, b * NG * G
                gate_up(ub, hb, 0, norm_of=(3 + b, (b + 3) % NB))
                with dve.Fori(0, NG // 2) as j:
                    gate_up(ub + 8 + j * 24, hb + 4 + j * 8, 1)
                    down(b, ub + 16 + j * 24)
                    gate_up(ub + 20 + j * 24, hb + 8 + j * 8, 0)
                    down(b, ub + 28 + j * 24)
                if more:
                    rms_fill(b + 1)
                down(b, ub + 80, last=True)

            with dve.Fori(0, NB - 1) as b:
                b_block(b, True)
            b_block(NB - 1, False)

            nc.vector.memset(vp_h[:].bitcast(F32), 0.0).then_inc(vp_zero, 1)
            nc.vector.memset(vp_l[:].bitcast(F32), 0.0).then_inc(vp_zero, 1)
            dve.wait_ge(rope_in, 32)

            def rope(b, m, src):
                if not isinstance(m, int) or m >= 1:
                    dve.wait_ge(roped_lo, 10 * b + m)
                nc.vector.tensor_copy(rope_a[:], src).then_inc(rope_st, 1)
                dve.wait_ge(rope_st, (10 * b + m) * 3 + 1)
                tt(rope_b[:], src, cos_t[:], mul)
                nc.vector.stream_shuffle(rope_a[:], rope_a[:], [(d + HD // 2) % HD for d in range(HD)])\
                    .then_inc(rope_st, 1)
                dve.wait_ge(rope_st, (10 * b + m) * 3 + 2)
                tt(rope_a[:], rope_a[:], sin_t[:], mul).then_inc(rope_st, 1)
                dve.wait_ge(rope_st, (10 * b + m) * 3 + 3)
                tt(rope_b[:], rope_b[:], rope_a[:], add).then_inc(roped, 1)

            def rope_lo(b, m, lo, hi):
                dve.wait_ge(roped_hi, 10 * b + m + 1)
                tt(lo, rope_b[:], hi.bitcast(F32), sub).then_inc(roped_lo, 1)

            with dve.Fori(0, NB) as b:
                fill(8 + 2 * b, b)
                uc = C_U + b * C_N
                for n in range(12):
                    post(uc + n)
                    split_unit(uc + n + RING, n)
                    if n in (1, 2):
                        dve.wait_ge(freed_a, C_FA * b + n)
                        rope(b, n - 1, qf[:, n - 1, :])
                        rope_lo(b, n - 1, kt_l[:, n - 1, :], kt_h[:, n - 1, :])
                    if n == 5:
                        ln_centre(7 + b, (b + 3) % NB)
                    if n == 9:
                        ln_scale(7 + b, (b + 3) % NB)
                dve.wait_ge(freed_a, C_FA * (b + 1))
                for half in range(2):
                    for r in range(4):
                        dve.wait_ge(vp_hi, 8 * b + 4 * half + r + 1)
                        at = slice(V_POS[r], V_POS[r] + HD)
                        tt(vp_l[:, :, at], v_f[:, :, half * P + r * HD:half * P + r * HD + HD],
                           vp_h[:, :, at].bitcast(F32), sub).then_inc(vp_lo, 1)
                    with dve.Fori(0, 4) as j:
                        a = 8 * b + 4 * half + j
                        m = 2 + 4 * half + j
                        dve.wait_ge(xs_lo, (9 + 2 * b) * KC + 4 * half + j)
                        rope(b, m, qf[:, 4 * half + j, :])
                        rope_lo(b, m, qs_l[:], qs_h[:])

                        def choose(i):
                            t = i // 4
                            n = P * (t + 1)
                            s0 = 48 * a + (i if t < 2 else 8 + (i - 8) * 5)
                            dve.wait_ge(scored, 16 * a + i + 1)
                            if t < 2:
                                nc.vector.tensor_reduce(rmax[:, i:i + 1], banks[:, i % 4, 0:n], AX, ALU.max).then_inc(sel, 1)
                                dve.wait_ge(sel, s0 + 1)
                                ts(nbias[:, i:i + 1], rmax[:, i:i + 1], -SCALE, None, mul).then_inc(nb_ok, 1)
                                return
                            nch = n // CHUNK
                            cmax, top8, marked, pen_c = (z[i % 2] for z in (cmaxs, top8s, marks, pens_c))
                            nc.vector.tensor_reduce(cmax[:, 0:nch], banks[:, i % 4, 0:n].rearrange(
                                "p (c k) -> p c k", k=CHUNK), AX, ALU.max).then_inc(sel, 1)
                            dve.wait_ge(sel, s0 + 1)
                            turned_lo(i - 2)
                            nc.vector.max(top8, cmax[:, 0:nch]).then_inc(sel, 1)
                            dve.wait_ge(sel, s0 + 2)
                            ts(nbias[:, i:i + 1], top8[:, 0:1], -SCALE, None, mul)
                            nc.vector.match_replace(marked[:, 0:nch], top8, cmax[:, 0:nch], MARK).then_inc(sel, 1)
                            dve.wait_ge(sel, s0 + 3)
                            ts(pen_c[:, 0:nch], marked[:, 0:nch], MARK, NEG, ALU.is_lt, mul).then_inc(sel, 1)
                            dve.wait_ge(sel, s0 + 4)
                            dve.wait_ge(nb_ok, 16 * a + i)
                            mid = n - 2 * P
                            c0 = P // CHUNK
                            tt(pen[:, 0:mid].rearrange("p (c k) -> p c k", k=CHUNK),
                               old[:, 2 * P - mid:2 * P].rearrange("p (c k) -> p c k", k=CHUNK),
                               pen_c[:, c0:c0 + mid // CHUNK].unsqueeze(2).broadcast_to([P, mid // CHUNK, CHUNK]),
                               ALU.max).then_inc(sel, 1)
                            dve.wait_ge(sel, s0 + 5)
                            tt(banks[:, i % 4, P:P + mid], banks[:, i % 4, P:P + mid], pen[:, 0:mid], add)\
                                .then_inc(nb_ok, 1)

                        def turned_lo(i):
                            n = P * (i // 4 + 1)
                            dve.wait_ge(pt_hi, 16 * a + i + 1)
                            tt(pt_l[:, i % 2, 0:n], t_bank[i % 2][:, 0:n], pt_h[:, i % 2, 0:n].bitcast(F32), sub)\
                                .then_inc(pt_lo, 1)
                            if i % 4 == 3:
                                nc.vector.reciprocal(rinvs[i // 4 % 2].rearrange("p (r d) -> p r d", d=HD),
                                                     rsum[:, i - 3:i + 1].unsqueeze(2).broadcast_to([P, 4, HD]))\
                                    .then_inc(rinv_ok, 1)

                        for i in range(16):
                            choose(i)
                            if 2 <= i < 8:
                                turned_lo(i - 2)
                        turned_lo(14)
                        turned_lo(15)
                        dve.wait_ge(pv_ok, 16 * a + 16)
                        dve.wait_ge(r_copied, a + 1)
                        tt(rope_b[:], o_bank, rope_a[:], mul).then_inc(o_ok, 1)
                        dve.wait_ge(xs_hi, (9 + 2 * b) * KC + 4 * half + j + 1)
                        tt(xs_l[:, 4 * half + j, :], rope_b[:], xs_h[:, 4 * half + j, :].bitcast(F32), sub)\
                            .then_inc(xs_lo, 1)
                for n in range(12, 20):
                    post(uc + n)
                    xo = x[:, b, n - 12, :]
                    tt(xo, banks[:, n % RING, :], xo, add).then_inc(freed_v, 1)
                    split_unit(uc + n + RING, n)
                    add_chunk(8 + b, b, n - 12, C_FV + b * KC + n - 12 + 1)

            for b in range(NB):
                fill(16 + b, b)
                post(E_U + b)
                split_unit(E_U + b + RING, b)
                if b == 0:
                    ln_centre(11, NB - 1)
                if b == 1:
                    ln_scale(11, NB - 1)
            dve.wait_ge(bm_hi, 1)
            tt(bm_l[:], b_raw[:], bm_h[:].bitcast(F32), sub).then_inc(bm_lo, 1)
            steps = [0]

            def step(instruction):
                steps[0] += 1
                instruction.then_inc(rtv, 1)
                dve.wait_ge(rtv, steps[0])

            def by8(c):
                return rt[:, c:c + 64].rearrange("p (m e) -> p m e", e=NE)

            def each(c):
                return rt[:, c:c + 8].unsqueeze(2).broadcast_to([P, 8, NE])

            dve.wait_ge(rtp, 1)
            step(nc.vector.tensor_copy(by8(0), ln_bank[:, 0:8 * EW].rearrange("p (m e) -> p m e", e=EW)[:, :, RANK:EW]))
            step(nc.vector.tensor_copy(rt[:, 64:128], banks[:, 5, 0:64]))
            step(nc.vector.tensor_reduce(rt[:, 128:129], rt[:, 0:64], AX, ALU.max, apply_absolute_value=True))
            step(nc.vector.tensor_reduce(rt[:, 129:130], rt[:, 64:128], AX, ALU.max, apply_absolute_value=True))
            dve.wait_ge(rtg, 1)
            step(ts(rt[:, 132:134], rt[:, 130:132], 1e-6, None, ALU.max))
            step(nc.vector.reciprocal(rt[:, 134:136], rt[:, 132:134]))
            step(ts(rt[:, 136:138], rt[:, 134:136], 0.5, None, mul))
            step(ts(rt[:, 192:256], rt[:, 64:128], rt[:, 137:138], None, mul))
            step(stt(rt[:, 192:256], rt[:, 0:64], rt[:, 136:137], rt[:, 192:256], mul, add))
            step(nc.vector.tensor_reduce(rt[:, 384:392], by8(192), AX, ALU.max))
            step(tt(by8(256), by8(192), each(384), sub))
            dve.wait_ge(rta, 1)
            step(nc.vector.tensor_reduce(rt[:, 392:400], by8(320), AX, ALU.add))
            step(nc.vector.reciprocal(rt[:, 400:408], rt[:, 392:400]))
            step(tt(by8(448), by8(320), each(400), mul))
            for m in range(8):
                step(nc.vector.max(rt[:, 512 + 8 * m:520 + 8 * m], rt[:, 448 + 8 * m:456 + 8 * m]))
            step(tt(by8(576), by8(448), by8(512)[:, :, 1:2].broadcast_to([P, 8, NE]), sub))
            dve.wait_ge(rta, 2)
            step(ts(rt[:, 704:768], rt[:, 640:704], 1.0, None, add))
            step(nc.vector.reciprocal(rt[:, 640:704], rt[:, 704:768]))
            step(tt(rt[:, 704:768], rt[:, 640:704], rt[:, 448:512], mul))
            step(nc.vector.tensor_reduce(rt[:, 408:416], by8(704), AX, ALU.add))
            step(ts(rt[:, 416:424], rt[:, 408:416], 1e-9, None, add))
            step(nc.vector.reciprocal(rt[:, 424:432], rt[:, 416:424]))
            step(tt(by8(768), by8(704), each(424), mul))
            dve.wait_ge(rtp, 2)
            step(nc.vector.tensor_copy(rt[0:NE, 1024:1536], banks[0:NE, 5, :]))
            step(nc.vector.tensor_copy(rt[0:NE, 1536:2048], banks[0:NE, 7, :]))
            dve.wait_ge(rtp, 3)
            for m, bank in ((0, 4), (1, 6)):
                half = slice(m * 2 * T, (m + 1) * 2 * T)
                step(stt(zp[:, half].rearrange("p (n a) -> p n a", a=2), zh[0:RANK, half].rearrange("p (n a) -> p n a", a=2),
                         0.5, banks[0:RANK, bank, :].unsqueeze(2).broadcast_to([RANK, T, 2]), mul, mul))
            assert steps[0] == MIXED

            def f_block(b, ln, more):
                fill(20 + b, b)
                dve.wait_ge(zs_hi, b + 1)
                tt(zs_l[:], zp[:, bass.ds(b * T, T)], zs_h[:].bitcast(F32), sub).then_inc(zs_lo, 1)
                for n in range(F_N):
                    post(F_U + b * F_N + n)
                    xo = x[:, b, n, :]
                    stt(xo, banks[:, n % RING, :], bias1[:, n:n + 1], xo, add, add).then_inc(freed_v, 1)
                    if more or n < 4:
                        split_unit(F_U + b * F_N + n + RING, n)
                    add_chunk(12 + b, b, n, F_FV + b * KC + n + 1)
                    if ln and n == 1:
                        ln_centre(11 + b, b - 1)
                    if ln and n == 5:
                        ln_scale(11 + b, b - 1)
            f_block(0, False, True)
            with dve.Fori(1, NB - 1) as b:
                f_block(b, True, True)
            f_block(NB - 1, True, False)
            ln_centre(15, NB - 1)
            ln_scale(15, NB - 1)

        @block.tensor
        def _(pe):
            mm = nc.tensor.matmul
            passes = ((w_h, xs_h), (w_h, xs_l), (w_l, xs_h))

            def ln_mean(n):
                pe.wait_ge(summed, (n + 1) * 7)
                if not isinstance(n, int) or n >= 1:
                    pe.wait_ge(normed, n * KC)
                mm(ln_bank, ones[:], full_sum[:], start=True, stop=True).then_inc(mean_ok, 1)

            def ln_var(n):
                pe.wait_ge(sq_added, (n + 1) * 7)
                mm(ln_bank, ones[:], sq_sum[:], start=True, stop=True).then_inc(var_ok, 1)

            def product(u, n, m=P, fill=None, free=False, more=()):
                pe.wait_ge(unit_lo, u + 1)
                for k in range(KC):
                    if fill is not None:
                        pe.wait_ge(xs_lo, fill * KC + k + 1)
                    for c, (w, xs) in enumerate(passes):
                        last = mm(banks[0:m, n % RING, :], w[:, n % RING, k * P:k * P + m], xs[:, k, :],
                                  start=(k == 0 and c == 0), stop=(k == KC - 1 and c == 2 and not more))
                    if free and k < KC - 1:
                        last.then_inc(xs_free, 1)
                for c, (w, z) in enumerate(more):
                    last = mm(banks[0:m, n % RING, :], w, z, start=False, stop=(c == len(more) - 1))
                last.then_inc(unit_done, 1)

            pe.wait_ge(consts_in, 160)

            def a_block(b, ln):
                for n in range(A_N):
                    if not isinstance(b, int) or n >= RING:
                        pe.wait_ge(freed_v, b * A_N + n - RING + 1)
                    product(A_U + b * A_N + n, n, fill=b if n == 0 else None, free=n == A_N - 1)
                    if ln and n == 1:
                        ln_mean(b - 1)
                    if ln and n == 5:
                        ln_var(b - 1)
            a_block(0, False)
            with pe.Fori(1, NB) as b:
                a_block(b, True)

            def gate_up(u0, h0, freed, fill=None, norm=None):
                for n in range(2 * G):
                    if n < RING:
                        pe.wait_ge(freed_v, freed - RING + n + 1)
                        if norm is None:
                            pe.wait_ge(h_ok, h0 - RING // 2 + n // 2 + 1)
                    else:
                        pe.wait_ge(h_ok, h0 + (n - RING) // 2 + 1)
                    product(u0 + n, n, fill=fill if n == 0 else None)
                    if norm is not None and n == 1:
                        ln_mean(norm)
                    if norm is not None and n == 5:
                        ln_var(norm)

            def down(u0, h0, buf, freed, h_before=None):
                pe.wait_ge(h_lo, h0 + G)
                for q in range(4):
                    pe.wait_ge(unit_lo, u0 + q + 1)
                    for oo in range(2):
                        o = 2 * q + oo
                        if o < RING and h_before is not None:
                            pe.wait_ge(h_ok, h_before + G - RING // 2 + o // 2 + 1)
                        else:
                            pe.wait_ge(freed_v, freed - RING + o + 1)
                        for i in range(G):
                            w0 = (oo * G + i) * P
                            for c, (w, hs) in enumerate(((w_h, hs_h), (w_h, hs_l), (w_l, hs_h))):
                                last = mm(banks[:, o % RING, :], w[:, q, w0:w0 + P], hs[:, buf, i, :],
                                          start=(i == 0 and c == 0), stop=(i == G - 1 and c == 2))
                    last.then_inc(unit_done, 1)

            with pe.Fori(0, NB) as b:
                ub, hb, fv = B_U + b * B_N, b * NG * G, B_FV + b * B_FREED
                gate_up(ub, hb, fv, fill=4 + b, norm=3 + b)
                with pe.Fori(0, NG // 2) as j:
                    gate_up(ub + 8 + j * 24, hb + 4 + j * 8, fv + j * 16)
                    down(ub + 16 + j * 24, hb + j * 8, 0, fv + j * 16, h_before=hb + 4 + j * 8)
                    gate_up(ub + 20 + j * 24, hb + 8 + j * 8, fv + j * 16 + 8)
                    down(ub + 28 + j * 24, hb + 4 + j * 8, 1, fv + j * 16 + 8, h_before=hb + 8 + j * 8)
                down(ub + 80, hb + 24, 0, fv + 48)

            pe.wait_ge(rope_in, 32)
            with pe.Fori(0, NB) as b:
                uc = C_U + b * C_N
                for n in range(12):
                    if n < RING:
                        pe.wait_ge(freed_v, C_FV + b * KC + n - RING + 1)
                    else:
                        pe.wait_ge(freed_a, b * C_FA + n - RING + 1)
                    if n not in (2, 3):
                        product(uc + n, n, fill=8 + 2 * b if n == 0 else None)
                    elif n == 3:
                        pe.wait_ge(unit_lo, uc + 4)
                        for t in range(QT):
                            dst = banks[:, 2 + t // 2, t % 2 * 2 * P:(t % 2 + 1) * 2 * P]
                            for k in range(KC):
                                for c, (w, xs) in enumerate(passes):
                                    last = mm(dst, xs[:, k, t * P:(t + 1) * P], w[:, 2:4, k * P:(k + 1) * P],
                                              start=(k == 0 and c == 0), stop=(k == KC - 1 and c == 2))
                        last.then_inc(unit_done, 2)
                    if n == 3:
                        ln_mean(7 + b)
                    if n == 9:
                        ln_var(7 + b)
                for half in range(2):
                    with pe.Fori(0, 4) as j:
                        a = 8 * b + 4 * half + j
                        pe.wait_ge(freed_a, (b + 1) * C_FA)
                        pe.wait_ge(normed, (8 + b) * KC)
                        pe.wait_ge(vp_lo, 8 * b + 4 * half + 4)
                        pe.wait_ge(roped_lo, 10 * b + 3 + 4 * half + j)

                        def scores(i):
                            t, r = divmod(i, 4)
                            n = P * (t + 1)
                            if i >= 4:
                                pe.wait_ge(p_ok, 16 * a + i - 3)
                            q_at, rows = slice(t * P, n), slice(HD * r, HD * r + HD)
                            for c, (q, k) in enumerate(((qs_h, kt_h), (qs_h, kt_l), (qs_l, kt_h))):
                                mm(banks[:, i % 4, 0:n], q[rows, q_at], k[rows, half, 0:n], start=c == 0, stop=False)
                            mm(banks[:, i % 4, t * P:n], ident_b[:], causal_b[:], start=False, stop=True)\
                                .then_inc(scored, 1)

                        def turn(i):
                            pe.wait_ge(p_ok, 16 * a + i + 1)
                            if i >= 2:
                                pe.wait_ge(pt_lo, 16 * a + i - 1)
                            for kt in range(i // 4 + 1):
                                last = nc.tensor.transpose(t_bank[i % 2][:, kt * P:(kt + 1) * P],
                                                           prob[:, i % 2, kt * P:(kt + 1) * P], ident[:])
                            last.then_inc(turned, 1)

                        def values(i):
                            t, r = divmod(i, 4)
                            pe.wait_ge(pt_lo, 16 * a + i + 1)
                            for kt in range(t + 1):
                                for c, (v, p) in enumerate(((vp_h, pt_h), (vp_h, pt_l), (vp_l, pt_h))):
                                    last = mm(o_bank[:, t * P:(t + 1) * P], v[:, kt, V_WIN[r]:V_WIN[r] + P],
                                              p[:, i % 2, kt * P:(kt + 1) * P],
                                              start=(r == 0 and kt == 0 and c == 0), stop=(r == 3 and kt == t and c == 2))
                            last.then_inc(pv_ok, 1)
                            if r == 3:
                                pe.wait_ge(rinv_ok, 4 * a + t + 1)
                                nc.tensor.transpose(ln_bank[:, t * P:(t + 1) * P], rinvs[t % 2],
                                                    ident[:]).then_inc(rinv_t, 1)

                        for i in range(3):
                            scores(i)
                        for i in range(16):
                            turn(i)
                            if i + 3 < 16:
                                scores(i + 3)
                            if i >= 2:
                                values(i - 2)
                        values(14)
                        values(15)
                for n in range(12, 20):
                    if n >= 16:
                        pe.wait_ge(freed_v, C_FV + b * KC + n - 16 + 1)
                    product(uc + n, n, fill=9 + 2 * b if n == 12 else None)

            for b in range(NB):
                pe.wait_ge(freed_v, F_FV - RING + b + 1)
                product(E_U + b, b, fill=16 + b)
                if b == 0:
                    ln_mean(11)
                if b == 1:
                    ln_var(11)
            pe.wait_ge(late_in, 48)
            pe.wait_ge(freed_a, NB * C_FA + NB)
            pe.wait_ge(normed, 12 * KC)
            for m in range(8):
                last_of_pair = zh[:, m * 2 * P:(m + 1) * 2 * P].rearrange("p (n a) -> p n a", a=2)[:, :, 1]
                nc.tensor.transpose(ln_bank[:, m * EW:(m + 1) * EW], last_of_pair[0:EW, :], ident[0:EW, 0:EW])
            for m in range(8):
                last_of_pair = zh[:, m * 2 * P:(m + 1) * 2 * P].rearrange("p (n a) -> p n a", a=2)[:, :, 1]
                last = mm(banks[:, 5, m * NE:(m + 1) * NE], last_of_pair[0:RANK, :], li_t[:], start=True, stop=True)
            last.then_inc(rtp, 1)
            pe.wait_ge(rtv, WEIGHED)
            for m in range(8):
                last = nc.tensor.transpose(banks[0:NE, 5 + m // 4 * 2, m % 4 * P:(m % 4 + 1) * P],
                                           rt[:, 768 + m * NE:768 + (m + 1) * NE], ident[:])
            last.then_inc(rtp, 1)
            pe.wait_ge(rtv, TURNED_W)
            mm(banks[0:RANK, 4, :], li[:], rt[0:NE, 1024:1536], start=True, stop=True)
            mm(banks[0:RANK, 6, :], li[:], rt[0:NE, 1536:2048], start=True, stop=True).then_inc(rtp, 1)
            pe.wait_ge(bm_lo, 1)
            pe.wait_ge(rtv, MIXED)

            def f_block(b, ln):
                for n in range(F_N):
                    pe.wait_ge(freed_v, F_FV + b * F_N + n - RING + 1)
                    if n == 0:
                        pe.wait_ge(zs_lo, b + 1)
                    o = slice(n * P, (n + 1) * P)
                    product(F_U + b * F_N + n, n, fill=20 + b if n == 0 else None,
                            more=((bm_h[:, o], zs_h[:]), (bm_h[:, o], zs_l[:]), (bm_l[:, o], zs_h[:])))
                    if ln and n == 1:
                        ln_mean(11 + b)
                    if ln and n == 5:
                        ln_var(11 + b)
            f_block(0, False)
            with pe.Fori(1, NB) as b:
                f_block(b, True)
            ln_mean(15)
            ln_var(15)


def unit_of(w):
    return w.reshape(-1, P, w.shape[1] // P, P).transpose(0, 3, 2, 1).reshape(-1, P, w.shape[1])


def layout(i):
    f32 = np.float32
    units = [unit_of(i["L0_attn_weight"])]
    gate, up = unit_of(i["L0_ffn_gate_w"]), unit_of(i["L0_ffn_up_w"])
    dn = i["L0_ffn_down_w"].reshape(4, 2, P, NG, G, P).transpose(3, 0, 5, 1, 4, 2).reshape(NG, 4, P, D)

    def gu(g):
        return np.stack([gate[g * G:(g + 1) * G], up[g * G:(g + 1) * G]], 1).reshape(2 * G, P, D)
    units.append(gu(0))
    for g in range(1, NG):
        units += [gu(g), dn[g - 1]]
    units.append(dn[NG - 1])
    wq = i["L1_attn_wq"].reshape(2, 4, 4, HD, D).transpose(0, 2, 1, 3, 4).reshape(D, D)
    wo = i["L1_attn_wo"].reshape(D, 2, 4, 4, HD).transpose(0, 1, 3, 2, 4).reshape(D, D)
    units += [unit_of(i["L1_attn_wk"]), unit_of(i["L1_attn_wv"]), unit_of(wq), unit_of(wo)]
    e = np.zeros((1, P, KC, P), f32)
    e[0, :, :, 0:RANK] = i["L1_ffn_A"].reshape(KC, P, RANK).transpose(1, 0, 2)
    e[0, :, :, RANK:EW] = i["L1_ffn_W"][0:NE].reshape(NE, KC, P).transpose(2, 1, 0)
    units += [e.reshape(1, P, D), unit_of(i["L1_ffn_W"])]
    units = np.concatenate(units)
    assert units.shape == (N_UNITS, P, D)

    inv = (1.0 / f32(10000.0) ** (np.arange(0, HD, 2, dtype=f32) / f32(HD))).astype(f32)
    angle = np.arange(T, dtype=f32)[:, None] * inv[None, :]
    cos, sin = np.cos(angle).astype(f32).T, np.sin(angle).astype(f32).T
    sin = np.concatenate([-sin, sin])
    q, k = np.arange(P)[:, None], np.arange(P)[None, :]
    bias_e = np.zeros((P, 1), f32)
    bias_e[RANK:EW, 0] = i["L1_ffn_b"][0:NE]
    bf = mybir.dt.np(BF16)
    return {
        "units": units,
        "x": np.ascontiguousarray(i["L0_attn_x"].reshape(NB, T, KC, P).transpose(0, 3, 2, 1)),
        "ones": np.full((P, P), 1.0 / D, f32),
        "ident": np.eye(P, dtype=f32),
        "ident_b": np.eye(P).astype(bf),
        "causal_b": np.where(k > q, NEG, 0.0).astype(bf),
        "old": np.concatenate([np.full((P, P), NEG, f32), np.where(k > q, 0.0, NEG).astype(f32)], 1),
        "bias0": np.ascontiguousarray(i["L0_attn_bias"].reshape(KC, P).T),
        "lnw": np.ascontiguousarray(i["L0_ffn_ln_w"].reshape(KC, P).T),
        "bias1": np.ascontiguousarray(i["L1_ffn_b"].reshape(KC, P).T),
        "bias_e": bias_e,
        "eps": np.full((P, 1), LN_EPS, f32),
        "cos": np.tile(np.concatenate([cos, cos]), (4, 1)),
        "sin": np.tile(sin, (4, 1)),
        "bmat": i["L1_ffn_Bmat"],
        "li": i["L1_ffn_LiMEs"],
        "li_t": np.ascontiguousarray(i["L1_ffn_LiMEs"].T),
    }


def kernel(**inputs):
    import concourse.bacc as bacc
    from concourse.bass_utils import run_bass_kernel_spmd

    arrays = layout({name: np.asarray(a) for name, a in inputs.items()})
    nc = bacc.Bacc("TRN2", target_bir_lowering=False, num_devices=1)
    io = {name: nc.dram_tensor(f"in_{name}", a.shape, mybir.dt.from_np(a.dtype), kind="ExternalInput").ap()
          for name, a in arrays.items()}
    io["out"] = nc.dram_tensor("out_x", (NB, P, KC, T), F32, kind="ExternalOutput").ap()
    build(nc, io)
    r = run_bass_kernel_spmd(nc, [{f"in_{name}": a for name, a in arrays.items()}], core_ids=[0])
    return r.results[0]["out_x"].transpose(0, 3, 2, 1).reshape(NB, T, D)
```

```python
from contextlib import ExitStack

import numpy as np

import concourse.bass as bass
from concourse import mybir

P = 128
NB = 4
T = 512
D = 1024
KC = D // P
FF = 3584
G = 4
NG = FF // P // G
NH, NKV, HD = 32, 8, 32
QT = T // P
CHUNK, TOPK = 16, 8
NE, RANK = 8, 32
LN_EPS = 1e-5
SCALE = float(HD) ** -0.5
NEG = -1e38
MARK = 3e38

A_N, B_N, C_N, E_N, F_N = KC, NG * (2 * G + 4), 20, 1, KC
A_W = 0
B_W = A_W + A_N
C_W = B_W + B_N
E_W = C_W + C_N
F_W = E_W + E_N
N_UNITS = F_W + F_N
A_U = 0
B_U = A_U + NB * A_N
C_U = B_U + NB * B_N
E_U = C_U + NB * C_N
F_U = E_U + NB * E_N
RING = 4
B_FREED = NG * KC
B_FV = NB * KC
C_FV = B_FV + NB * B_FREED
F_FV = C_FV + NB * KC
C_FA = 12
EW = RANK + NE
MAXED, SHIFTED, ABOVE, WEIGHED, TURNED_W, MIXED = 4, 11, 23, 30, 32, 34
V_POS = [0, 128, 224, 352]
V_WIN = [V_POS[r] - HD * r for r in range(4)]
V_ROW = 384
PT_AT = [0, 7, 5, 4]
PT_W = 10 * P
TURN_ORDER = [[0], [0, 1], [0, 2, 1], [0, 2, 1, 3]]

SCRATCH = 2048

ALU = mybir.AluOpType
ACT = mybir.ActivationFunctionType
AX = mybir.AxisListType.X
F32 = mybir.dt.float32
F32R = mybir.dt.float32r
BF16 = mybir.dt.bfloat16
RMAX = bass.bass_isa.ReduceOp.max


def build(nc, io):
    with ExitStack() as ctx:
        def sb(name, shape, dt=F32):
            return ctx.enter_context(nc.sbuf_tensor(name, shape, dt))

        def sem(name):
            return ctx.enter_context(nc.semaphore(name))

        x = sb("x", [P, NB, KC, T])
        xs_h = sb("xs_h", [P, KC, T], F32R)
        xs_l = sb("xs_l", [P, KC, T], F32R)
        raw = sb("raw", [P, 2, KC * P])
        w_h = sb("w_h", [P, RING, KC * P], F32R)
        w_l = sb("w_l", [P, RING, KC * P], F32R)
        full_sum = sb("full_sum", [P, T])
        ones = sb("ones", [P, P])
        ident = sb("ident", [P, P])
        ident_b = sb("ident_b", [P, P], BF16)
        causal_b = sb("causal_b", [P, P], BF16)
        old = sb("old", [P, 2 * P])
        bias0 = sb("bias0", [P, KC])
        lnw = sb("lnw", [P, KC])
        bias1 = sb("bias1", [P, KC])
        bias_e = sb("bias_e", [P, 1])
        eps = sb("eps", [P, 1])

        def place(*tensors):
            with ExitStack() as own:
                return [own.enter_context(nc.sbuf_tensor(n, s, d)) for n, s, d in tensors]

        sq, sq_sum, sd, rstd, part_sum = place(
            ("sq", [P, 2, T], F32), ("sq_sum", [P, T], F32), ("sd", [P, T], F32), ("rstd", [P, T], F32),
            ("part_sum", [P, T], F32))
        prob, pt_h, pt_l = place(("prob", [P, 2, T], F32), ("pt_h", [P, 2, PT_W], F32R), ("pt_l", [P, 2, PT_W], F32R))
        sb("norm_or_attention", [P, 2 * T + 4 * PT_W])
        hs_h, hs_l, h_raw, silu_g, var_x, nx, r_rms = place(
            ("hs_h", [P, 2, G, T], F32R), ("hs_l", [P, 2, G, T], F32R), ("h_raw", [P, 2, T], F32),
            ("silu_g", [P, 2, T], F32), ("var_x", [P, NB, T], F32), ("nx", [P, 2, T], F32),
            ("r_rms", [P, T], F32))
        vp_h, vp_l, kt_h, kt_l, qf, v_f, qs_h, qs_l, rope_a, rope_b, cos_t, sin_t, small = place(
            ("vp_h", [P, QT, V_ROW], F32R), ("vp_l", [P, QT, V_ROW], F32R),
            ("kt_h", [P, 2, T], F32R), ("kt_l", [P, 2, T], F32R), ("qf", [P, KC, T], F32),
            ("v_f", [P, QT, 2 * P], F32), ("qs_h", [P, T], F32R), ("qs_l", [P, T], F32R),
            ("rope_a", [P, T], F32), ("rope_b", [P, T], F32), ("cos_t", [P, T], F32),
            ("sin_t", [P, T], F32), ("small", [P, 1088], F32))
        zh, zp, zs_h, zs_l, b_raw, bm_h, bm_l, li, li_t, rt = place(
            ("zh", [P, NB * T], F32), ("zp", [RANK, NB * T], F32), ("zs_h", [RANK, T], F32R),
            ("zs_l", [RANK, T], F32R), ("b_raw", [RANK, D], F32), ("bm_h", [RANK, D], F32R),
            ("bm_l", [RANK, D], F32R), ("li", [NE, RANK], F32), ("li_t", [RANK, NE], F32),
            ("rt", [P, 1024 + NB * T // 2], F32))

        def two(at, n):
            return [small[:, at:at + n], small[:, at + n:at + 2 * n]]

        cmaxs, top8s, marks = two(0, 32), two(64, 8), two(80, 32)
        pens, rinvs = [small[:, 144:272], small[:, 272:528]], small[:, 528:1040]
        nbias, rsum, rmax = small[:, 1040:1056], small[:, 1056:1072], small[:, 1072:1088]

        swapped = [rope_a[:], rinvs]

        banks = ctx.enter_context(nc.psum_tensor("banks", [P, 8, 512], F32))
        ln_bank, o_bank = banks[:, 4, :], banks[:, 6, :]
        t_bank = [banks[:, 5, :], banks[:, 7, :]]

        def turned_tiles(dst, r, t, i):
            tiles = dst[:, r % 2, :].rearrange("p (u q) -> p u q", q=P)
            src = t_bank[i % 2].rearrange("p (u q) -> p u q", q=P)
            m = min(t + 1, 3)
            gap = 6 if t == 1 else 3
            pairs = [(tiles[:, t:t + (m - 1) * gap + 1:gap, :] if m > 1 else tiles[:, t:t + 1, :], src[:, 0:m, :])]
            if t == 3:
                pairs.append((tiles[:, 4:5, :], src[:, 3:4, :]))
            return pairs

        x0_in = [sem(f"x0_in{k}") for k in range(KC)]
        x_in = sem("x_in")
        consts_in = sem("consts_in")
        rope_in = sem("rope_in")
        late_in = sem("late_in")
        raw_in = [sem(f"raw_in{i}") for i in range(2)]
        unit_hi = sem("unit_hi")
        unit_lo = sem("unit_lo")
        unit_done = sem("unit_done")
        xs_hi = sem("xs_hi")
        xs_lo = sem("xs_lo")
        xs_free = sem("xs_free")
        freed_v = sem("freed_v")
        freed_a = sem("freed_a")
        summed = sem("summed")
        mean_ok = sem("mean_ok")
        centred = sem("centred")
        squared = sem("squared")
        sq_added = sem("sq_added")
        var_ok = sem("var_ok")
        sd_ok = sem("sd_ok")
        rstd_ok = sem("rstd_ok")
        normed = sem("normed")
        ms_half = sem("ms_half")
        ms_ok = sem("ms_ok")
        rms_root = sem("rms_root")
        rms_ok = sem("rms_ok")
        nx_ok = sem("nx_ok")
        silu_ok = sem("silu_ok")
        h_ok = sem("h_ok")
        h_hi = sem("h_hi")
        h_lo = sem("h_lo")
        rope_st = sem("rope_st")
        roped = sem("roped")
        roped_hi = sem("roped_hi")
        roped_lo = sem("roped_lo")
        q_shuffled = sem("q_shuffled")
        q_sin = sem("q_sin")
        q_roped = sem("q_roped")
        q_hi = sem("q_hi")
        q_lo = sem("q_lo")
        rinv_s = sem("rinv_s")
        vp_zero = sem("vp_zero")
        vp_hi = sem("vp_hi")
        vp_lo = sem("vp_lo")
        scored = sem("scored")
        sel = sem("sel")
        nb_ok = sem("nb_ok")
        p_ok = sem("p_ok")
        turned = sem("turned")
        pt_hi = sem("pt_hi")
        pt_lo = sem("pt_lo")
        pv_ok = sem("pv_ok")
        rinv_ok = sem("rinv_ok")
        rinv_t = sem("rinv_t")
        o_ok = sem("o_ok")
        r_copied = sem("r_copied")
        z_ok = sem("z_ok")
        rtp = sem("rtp")
        rtv = sem("rtv")
        rta = sem("rta")
        rtg = sem("rtg")
        bm_hi = sem("bm_hi")
        bm_lo = sem("bm_lo")
        zs_hi = sem("zs_hi")
        zs_lo = sem("zs_lo")
        out_done = sem("out_done")
        block = ctx.enter_context(nc.Block())


        @block.sync
        def _(sp):
            def load(u, slot, src):
                sp.dma_start(raw[:, slot, :], io["units"][src]).then_inc(raw_in[slot], 16)

            def pair(u, src):
                for s in range(2):
                    sp.wait_ge(unit_lo, u + s - 1)
                    load(u + s, s, src + s)

            load(0, 0, A_W)
            load(1, 1, A_W + 1)
            for n in range(2, A_N, 2):
                pair(n, A_W + n)
            with sp.Fori(1, NB) as b:
                with sp.Fori(0, A_N // 2) as n:
                    pair(A_U + b * A_N + n * 2, A_W + n * 2)
            for base, count, src in ((B_U, B_N, B_W), (C_U, C_N, C_W)):
                with sp.Fori(0, NB) as b:
                    with sp.Fori(0, count // 2) as n:
                        pair(base + b * count + n * 2, src + n * 2)
            for b in range(NB):
                sp.wait_ge(unit_lo, E_U + b - 1)
                load(E_U + b, b % 2, E_W)
            with sp.Fori(0, NB) as b:
                with sp.Fori(0, F_N // 2) as n:
                    pair(F_U + b * F_N + n * 2, F_W + n * 2)
            with sp.Fori(0, NB) as b:
                sp.wait_ge(normed, (12 + b + 1) * KC)
                sp.dma_start(io["out"][b], x[:, b, :, :]).then_inc(out_done, 16)
            sp.wait_ge(out_done, 16 * NB)

        @block.gpsimd
        def _(pool):
            tt = nc.gpsimd.tensor_tensor
            pool.wait_ge(rope_in, 32)
            with pool.Fori(0, NB) as b:
                for c in range(KC):
                    pool.wait_ge(q_shuffled, 8 * b + c + 1)
                    tt(qf[:, c, :], qf[:, c, :], cos_t[:], ALU.mult)
                    tt(swapped[c % 2], swapped[c % 2], sin_t[:], ALU.mult).then_inc(q_sin, 1)
                    pool.wait_ge(q_sin, 8 * b + c + 1)
                    tt(qf[:, c, :], qf[:, c, :], swapped[c % 2], ALU.add).then_inc(q_roped, 1)

            pool.wait_ge(rtv, MAXED)
            nc.gpsimd.partition_all_reduce(rt[:, 130:132], rt[:, 128:130], P, RMAX).then_inc(rtg, 1)

        @block.scalar
        def _(act):
            for k in range(KC):
                act.dma_start(x[:, 0, k, :], io["x"][0, :, k, :]).then_inc(x0_in[k], 16)
            for dst, name in ((ones, "ones"), (ident, "ident"), (ident_b, "ident_b"), (causal_b, "causal_b"),
                              (old, "old"), (bias0, "bias0"), (lnw, "lnw"), (bias1, "bias1"),
                              (bias_e, "bias_e"), (eps, "eps")):
                act.dma_start(dst[:], io[name]).then_inc(consts_in, 16)
            for b in range(1, NB):
                act.dma_start(x[:, b, :, :], io["x"][b]).then_inc(x_in, 16)
            copy = ACT.Copy

            def split_unit(u, n):
                act.wait_ge(raw_in[n % 2], 8 * (u - n % 2) + 16)
                if not isinstance(u, int) or u >= RING:
                    act.wait_ge(unit_done, u - RING + 1)
                nc.scalar.activation(w_h[:, n % RING, :], raw[:, n % 2, :], copy).then_inc(unit_hi, 1)

            def post(u):
                act.wait_ge(unit_done, u + 1)

            def ln_squares(n, p):
                for k in range(KC):
                    act.wait_ge(centred, n * KC + k + 1)
                    if k >= 2:
                        act.wait_ge(sq_added, n * 7 + max(1, k - 2))
                    nc.scalar.activation(sq[:, k % 2, :], x[:, p, k, :], ACT.Square).then_inc(squared, 1)

            def ln_root(n):
                act.wait_ge(var_ok, n + 1)
                nc.scalar.activation(sd[:], ln_bank, ACT.Sqrt, bias=eps[:]).then_inc(sd_ok, 1)

            def chunk_free(b, k):
                if k < KC - 1:
                    act.wait_ge(xs_free, b * (KC - 1) + k + 1)
                else:
                    act.wait_ge(unit_done, A_U + (b + 1) * A_N)

            def fill(b, ready):
                for k in range(KC):
                    ready(k)
                    nc.scalar.activation(xs_h[:, k, :], x[:, b, k, :], copy).then_inc(xs_hi, 1)

            for n in range(RING):
                split_unit(n, n)
                if n == 0:
                    fill(0, lambda k: act.wait_ge(x0_in[k], 16))
            act.wait_ge(consts_in, 160)

            def a_block(b, ln, more):
                for n in range(A_N):
                    if n == A_N - 1 and more:
                        act.wait_ge(x_in, 16 * (NB - 1))
                        fill(b + 1, lambda k: chunk_free(b, k))
                    elif n == A_N - 1:
                        rms_fill(0, free=lambda k: chunk_free(NB - 1, k))
                    post(A_U + b * A_N + n)
                    split_unit(A_U + b * A_N + n + RING, n)
                    if ln and n == 1:
                        ln_squares(b - 1, b - 1)
                    if ln and n == 5:
                        ln_root(b - 1)

            def rms_fill(b, free=lambda k: None):
                act.wait_ge(ms_ok, b + 1)
                nc.scalar.activation(r_rms[:], var_x[:, b, :], ACT.Sqrt, bias=eps[:]).then_inc(rms_root, 1)
                for k in range(KC):
                    free(k)
                    act.wait_ge(nx_ok, b * KC + k + 1)
                    nc.scalar.activation(xs_h[:, k, :], nx[:, k % 2, :], copy, scale=lnw[:, k:k + 1]).then_inc(xs_hi, 1)

            a_block(0, False, True)
            with act.Fori(1, NB - 1) as b:
                a_block(b, True, True)
            a_block(NB - 1, True, False)

            def gate_up(u0, h0, buf, norm_of=None):
                for i in range(G):
                    post(u0 + 2 * i)
                    if i >= 2 or norm_of is None:
                        act.wait_ge(h_ok, h0 + i - 1)
                    nc.scalar.activation(silu_g[:, i % 2, :], banks[:, 2 * i % RING, :], ACT.Silu).then_inc(silu_ok, 1)
                    split_unit(u0 + 2 * i + RING, 2 * i)
                    act.wait_ge(h_ok, h0 + i + 1)
                    nc.scalar.activation(hs_h[:, buf, i, :], h_raw[:, i % 2, :], copy).then_inc(h_hi, 1)
                    post(u0 + 2 * i + 1)
                    split_unit(u0 + 2 * i + 1 + RING, 2 * i + 1)
                    if norm_of is not None and i == 0:
                        ln_squares(*norm_of)
                    if norm_of is not None and i == 2:
                        ln_root(norm_of[0])

            def down(u0):
                for q in range(4):
                    post(u0 + q)
                    split_unit(u0 + q + RING, q)

            def b_block(b, more):
                ub, hb = B_U + b * B_N, b * NG * G
                gate_up(ub, hb, 0, norm_of=(3 + b, (b + 3) % NB))
                with act.Fori(0, NG // 2) as j:
                    gate_up(ub + 8 + j * 24, hb + 4 + j * 8, 1)
                    down(ub + 16 + j * 24)
                    gate_up(ub + 20 + j * 24, hb + 8 + j * 8, 0)
                    down(ub + 28 + j * 24)
                if more:
                    rms_fill(b + 1)
                down(ub + 80)

            with act.Fori(0, NB - 1) as b:
                b_block(b, True)
            b_block(NB - 1, False)

            act.dma_start(cos_t[:], io["cos"]).then_inc(rope_in, 16)
            act.dma_start(sin_t[:], io["sin"]).then_inc(rope_in, 16)
            act.wait_ge(vp_zero, 2)
            with act.Fori(0, NB) as b:
                fill(b, lambda k: act.wait_ge(normed, (4 + b) * KC + k + 1))
                uc = C_U + b * C_N
                for n in range(12):
                    post(uc + n)
                    if n in (2, 3):
                        v_dst = v_f[:, 2 * (n - 2):2 * (n - 2) + 2, :].rearrange("p t c -> p (t c)")
                        nc.scalar.activation(v_dst, banks[:, n, :], copy).then_inc(freed_a, 1)
                    else:
                        if n in (4, 5):
                            act.wait_ge(roped, 2 * b + n - 3)
                        nc.scalar.activation(qf[:, n if n < 2 else n - 4, :], banks[:, n % RING, :], copy)\
                            .then_inc(freed_a, 1)
                    split_unit(uc + n + RING, n)
                    if n in (1, 2):
                        act.wait_ge(roped, 2 * b + n)
                        nc.scalar.activation(kt_h[:, n - 1, :], rope_b[:], copy).then_inc(roped_hi, 1)
                    if n == 5:
                        ln_squares(7 + b, (b + 3) % NB)
                    if n == 9:
                        ln_root(7 + b)
                for half in range(2):
                    for r in range(4):
                        nc.scalar.activation(vp_h[:, :, V_POS[r]:V_POS[r] + HD],
                                             v_f[:, :, half * P + r * HD:half * P + r * HD + HD], copy)\
                            .then_inc(vp_hi, 1)

                    def split_queries(j):
                        act.wait_ge(q_roped, 8 * b + 4 * half + j + 1)
                        nc.scalar.activation(qs_h[:], qf[:, 4 * half + j, :], copy).then_inc(q_hi, 1)

                    def turned_hi(a, i):
                        r, t = divmod(i % 16, 4)
                        act.wait_ge(turned, 16 * a + i + 1)
                        for piece, (dst, src) in enumerate(turned_tiles(pt_h, r, t, i)):
                            last = nc.scalar.activation(dst, src, copy)
                        last.then_inc(pt_hi, 1)

                    def four_heads(j, first=False, last=False):
                        a = 8 * b + 4 * half + j
                        def exp(i):
                            n = P * (i % 4 + 1)
                            act.wait_ge(nb_ok, 16 * a + i + 1)
                            if i >= 2 or not first:
                                act.wait_ge(turned, 16 * a + i - 1)
                            nc.scalar.activation(prob[:, i % 2, 0:n], banks[:, i % 4, 0:n], ACT.Exp,
                                                 bias=nbias[:, i:i + 1], scale=SCALE,
                                                 accum_out=rsum[:, i % 4 * 4 + i // 4:i % 4 * 4 + i // 4 + 1])\
                                .then_inc(p_ok, 1)

                        for i in range(16):
                            if i % 4 != 2:
                                exp(i)
                            if i >= 1 or not first:
                                if (i - 1) % 4 == 0 and (i >= 9 or not first):
                                    act.wait_ge(pv_ok, 4 * a + (i - 1) // 4 - 1)
                                turned_hi(a, i - 1)
                            if i % 4 == 2:
                                exp(i)
                            if i == 13 and not last:
                                act.wait_ge(scored, 16 * a + 16)
                                split_queries(j + 1)
                            if i == 3 and not first:
                                factors(a - 1)
                            if i == 5 and not first:
                                output(j - 1)

                    def factors(a):
                        act.wait_ge(q_roped, 8 * b + KC)
                        act.wait_ge(rinv_t, a + 1)
                        nc.scalar.activation(rope_a[:], ln_bank, copy).then_inc(r_copied, 1)

                    def output(j):
                        act.wait_ge(o_ok, 8 * b + 4 * half + j + 1)
                        nc.scalar.activation(xs_h[:, 4 * half + j, :], rope_b[:], copy).then_inc(xs_hi, 1)

                    split_queries(0)
                    four_heads(0, first=True)
                    with act.Fori(1, 3) as j:
                        four_heads(j)
                    four_heads(3, last=True)
                    turned_hi(8 * b + 4 * half + 4, -1)
                    factors(8 * b + 4 * half + 3)
                    output(3)
                for n in range(12, 20):
                    post(uc + n)
                    split_unit(uc + n + RING, n)

            act.dma_start(b_raw[:], io["bmat"]).then_inc(late_in, 16)
            act.dma_start(li[:], io["li"]).then_inc(late_in, 16)
            act.dma_start(li_t[:], io["li_t"]).then_inc(late_in, 16)
            for b in range(NB):
                fill(b, lambda k: act.wait_ge(normed, (8 + b) * KC + k + 1))
                post(E_U + b)
                nc.scalar.activation(zh[0:EW, b * T:(b + 1) * T], banks[0:EW, b, :], ACT.Identity,
                                     bias=bias_e[0:EW, :]).then_inc(freed_a, 1)
                split_unit(E_U + b + RING, b)
                if b == 0:
                    ln_squares(11, NB - 1)
                if b == 1:
                    ln_root(11)
            act.wait_ge(late_in, 48)
            nc.scalar.activation(bm_h[:], b_raw[:], copy).then_inc(bm_hi, 1)
            act.wait_ge(rtv, SHIFTED)
            nc.scalar.activation(rt[:, 320:384], rt[:, 256:320], ACT.Exp).then_inc(rta, 1)
            act.wait_ge(rtv, ABOVE)
            nc.scalar.activation(rt[:, 640:704], rt[:, 576:640], ACT.Exp, scale=-2.0).then_inc(rta, 1)
            act.wait_ge(rtv, MIXED)

            def f_block(b, ln, more):
                fill(b, lambda k: None)
                nc.scalar.activation(zs_h[:], zp[:, bass.ds(b * T, T)], copy).then_inc(zs_hi, 1)
                for n in range(F_N):
                    post(F_U + b * F_N + n)
                    if more or n < 4:
                        split_unit(F_U + b * F_N + n + RING, n)
                    if ln and n == 1:
                        ln_squares(11 + b, b - 1)
                    if ln and n == 5:
                        ln_root(11 + b)
            f_block(0, False, True)
            with act.Fori(1, NB - 1) as b:
                f_block(b, True, True)
            f_block(NB - 1, True, False)
            ln_squares(15, NB - 1)
            ln_root(15)

        @block.vector
        def _(dve):
            tt = nc.vector.tensor_tensor
            ts = nc.vector.tensor_scalar
            stt = nc.vector.scalar_tensor_tensor
            sub, add, mul = ALU.subtract, ALU.add, ALU.mult

            def split_unit(u, n):
                dve.wait_ge(unit_hi, u + 1)
                tt(w_l[:, n % RING, :], raw[:, n % 2, :], w_h[:, n % RING, :].bitcast(F32), sub).then_inc(unit_lo, 1)

            def fill(f, b):
                for k in range(KC):
                    dve.wait_ge(xs_hi, f * KC + k + 1)
                    tt(xs_l[:, k, :], x[:, b, k, :], xs_h[:, k, :].bitcast(F32), sub).then_inc(xs_lo, 1)

            def rms_fill(b):
                dve.wait_ge(rms_root, b + 1)
                nc.vector.reciprocal(r_rms[:], r_rms[:]).then_inc(rms_ok, 1)
                dve.wait_ge(rms_ok, b + 1)

                def lo(k):
                    dve.wait_ge(xs_hi, (4 + b) * KC + k + 1)
                    stt(xs_l[:, k, :], nx[:, k % 2, :], lnw[:, k:k + 1], xs_h[:, k, :].bitcast(F32), mul, sub)\
                        .then_inc(xs_lo, 1)
                for k in range(KC):
                    if k >= 2:
                        dve.wait_ge(xs_lo, (4 + b) * KC + k - 1)
                    tt(nx[:, k % 2, :], x[:, b, k, :], r_rms[:], mul).then_inc(nx_ok, 1)
                    if k >= 1:
                        lo(k - 1)
                lo(KC - 1)

            def post(u):
                dve.wait_ge(unit_done, u + 1)

            def add_chunk(n, b, o, freed):
                if o == 0:
                    return
                dve.wait_ge(freed_v, freed)
                if o >= 2:
                    dve.wait_ge(summed, n * 7 + o - 1)
                dst = full_sum if o == KC - 1 else part_sum
                tt(dst[:], x[:, b, o, :], x[:, b, 0, :] if o == 1 else part_sum[:], add).then_inc(summed, 1)

            def ln_centre(n, p):
                dve.wait_ge(mean_ok, n + 1)
                for k in range(KC):
                    tt(x[:, p, k, :], x[:, p, k, :], ln_bank, sub).then_inc(centred, 1)
                for k in range(1, KC):
                    dve.wait_ge(squared, n * KC + k + 1)
                    if k >= 2:
                        dve.wait_ge(sq_added, n * 7 + k - 1)
                    tt(sq_sum[:], sq[:, k % 2, :], sq[:, 0, :] if k == 1 else sq_sum[:], add).then_inc(sq_added, 1)

            def ln_scale(n, p, keep=False):
                dve.wait_ge(sd_ok, n + 1)
                nc.vector.reciprocal(rstd[:], sd[:]).then_inc(rstd_ok, 1)
                dve.wait_ge(rstd_ok, n + 1)
                if keep:
                    tt(var_x[:, p, :], rstd[:], ln_bank, mul).then_inc(ms_half, 1)
                for k in range(KC):
                    tt(x[:, p, k, :], x[:, p, k, :], rstd[:], mul).then_inc(normed, 1)
                if keep:
                    dve.wait_ge(ms_half, n + 1)
                    tt(var_x[:, p, :], var_x[:, p, :], rstd[:], mul).then_inc(ms_ok, 1)

            for n in range(RING):
                split_unit(n, n)
                if n == 0:
                    fill(0, 0)
            dve.wait_ge(consts_in, 160)

            def a_block(b, ln, more):
                for n in range(A_N):
                    if n == A_N - 1:
                        fill(b + 1, b + 1) if more else rms_fill(0)
                    post(A_U + b * A_N + n)
                    xo = x[:, b, n, :]
                    stt(xo, banks[:, n % RING, :], bias0[:, n:n + 1], xo, add, add).then_inc(freed_v, 1)
                    split_unit(A_U + b * A_N + n + RING, n)
                    add_chunk(b, b, n, b * KC + n + 1)
                    if ln and n == 1:
                        ln_centre(b - 1, b - 1)
                    if ln and n == 5:
                        ln_scale(b - 1, b - 1, keep=True)

            a_block(0, False, True)
            with dve.Fori(1, NB - 1) as b:
                a_block(b, True, True)
            a_block(NB - 1, True, False)

            def gate_up(u0, h0, buf, norm_of=None):
                def lo(i):
                    dve.wait_ge(h_hi, h0 + i + 1)
                    tt(hs_l[:, buf, i, :], h_raw[:, i % 2, :], hs_h[:, buf, i, :].bitcast(F32), sub).then_inc(h_lo, 1)
                for i in range(G):
                    post(u0 + 2 * i)
                    split_unit(u0 + 2 * i + RING, 2 * i)
                    post(u0 + 2 * i + 1)
                    dve.wait_ge(silu_ok, h0 + i + 1)
                    tt(h_raw[:, i % 2, :], banks[:, (2 * i + 1) % RING, :], silu_g[:, i % 2, :], mul).then_inc(h_ok, 1)

                    split_unit(u0 + 2 * i + 1 + RING, 2 * i + 1)
                    lo(i)
                    if norm_of is not None and i == 0:
                        ln_centre(*norm_of)
                    if norm_of is not None and i == 2:
                        ln_scale(*norm_of, keep=True)

            def down(b, u0, last=False):
                for q in range(4):
                    post(u0 + q)
                    for o in (2 * q, 2 * q + 1):
                        xo = x[:, b, o, :]
                        tt(xo, banks[:, o % RING, :], xo, add).then_inc(freed_v, 1)
                    split_unit(u0 + q + RING, q)
                    if last:
                        for o in (2 * q, 2 * q + 1):
                            add_chunk(4 + b, b, o, B_FV + (b + 1) * B_FREED - KC + o + 1)

            def b_block(b, more):
                ub, hb = B_U + b * B_N, b * NG * G
                gate_up(ub, hb, 0, norm_of=(3 + b, (b + 3) % NB))
                with dve.Fori(0, NG // 2) as j:
                    gate_up(ub + 8 + j * 24, hb + 4 + j * 8, 1)
                    down(b, ub + 16 + j * 24)
                    gate_up(ub + 20 + j * 24, hb + 8 + j * 8, 0)
                    down(b, ub + 28 + j * 24)
                if more:
                    rms_fill(b + 1)
                down(b, ub + 80, last=True)

            with dve.Fori(0, NB - 1) as b:
                b_block(b, True)
            b_block(NB - 1, False)

            nc.vector.memset(vp_h[:].bitcast(F32), 0.0).then_inc(vp_zero, 1)
            nc.vector.memset(vp_l[:].bitcast(F32), 0.0).then_inc(vp_zero, 1)
            dve.wait_ge(rope_in, 32)

            swap = [(d + HD // 2) % HD for d in range(HD)]

            def rope_keys(b, c):
                s0 = (2 * b + c) * 2
                tt(rope_b[:], qf[:, c, :], cos_t[:], mul)
                nc.vector.stream_shuffle(rope_a[:], qf[:, c, :], swap).then_inc(rope_st, 1)
                dve.wait_ge(rope_st, s0 + 1)
                tt(rope_a[:], rope_a[:], sin_t[:], mul).then_inc(rope_st, 1)
                dve.wait_ge(rope_st, s0 + 2)
                tt(rope_b[:], rope_b[:], rope_a[:], add).then_inc(roped, 1)

            with dve.Fori(0, NB) as b:
                fill(8 + 2 * b, b)
                uc = C_U + b * C_N
                for n in range(12):
                    post(uc + n)
                    c = n - 4
                    if c >= 2:
                        dve.wait_ge(q_roped, 8 * b + c - 1)
                    if c >= 0:
                        dve.wait_ge(freed_a, C_FA * b + n + 1)
                    split_unit(uc + n + RING, n)
                    if c >= 0:
                        nc.vector.stream_shuffle(swapped[c % 2], qf[:, c, :], swap).then_inc(q_shuffled, 1)
                    if n in (1, 2):
                        dve.wait_ge(freed_a, C_FA * b + n)
                        if n == 2:
                            dve.wait_ge(roped_lo, 2 * b + 1)
                        rope_keys(b, n - 1)
                        dve.wait_ge(roped_hi, 2 * b + n)
                        tt(kt_l[:, n - 1, :], rope_b[:], kt_h[:, n - 1, :].bitcast(F32), sub).then_inc(roped_lo, 1)
                    if n == 5:
                        ln_centre(7 + b, (b + 3) % NB)
                    if n == 9:
                        ln_scale(7 + b, (b + 3) % NB)
                for half in range(2):
                    for r in range(4):
                        dve.wait_ge(vp_hi, 8 * b + 4 * half + r + 1)
                        at = slice(V_POS[r], V_POS[r] + HD)
                        tt(vp_l[:, :, at], v_f[:, :, half * P + r * HD:half * P + r * HD + HD],
                           vp_h[:, :, at].bitcast(F32), sub).then_inc(vp_lo, 1)

                    def queries_lo(j):
                        dve.wait_ge(q_hi, 8 * b + 4 * half + j + 1)
                        tt(qs_l[:], qf[:, 4 * half + j, :], qs_h[:].bitcast(F32), sub).then_inc(q_lo, 1)

                    def four_heads(j, first=False, last=False):
                        a = 8 * b + 4 * half + j

                        def largest(i):
                            n = P * (i % 4 + 1)
                            s0 = 40 * a + 10 * (i // 4) + i % 4
                            dve.wait_ge(scored, 16 * a + i + 1)
                            nc.vector.tensor_reduce(rmax[:, i:i + 1], banks[:, i % 4, 0:n], AX, ALU.max).then_inc(sel, 1)
                            dve.wait_ge(sel, s0 + 1)
                            ts(nbias[:, i:i + 1], rmax[:, i:i + 1], -SCALE, None, mul).then_inc(nb_ok, 1)

                        def choose(r):
                            s0 = 40 * a + 10 * r + 2
                            pair = [(4 * r + t, t - 2, P * (t + 1), P * (t + 1) // CHUNK) for t in (2, 3)]
                            for i, c, n, nch in pair:
                                dve.wait_ge(scored, 16 * a + i + 1)
                                nc.vector.tensor_reduce(cmaxs[c][:, 0:nch], banks[:, i % 4, 0:n].rearrange(
                                    "p (c k) -> p c k", k=CHUNK), AX, ALU.max).then_inc(sel, 1)
                            dve.wait_ge(sel, s0 + 2)
                            turned_lo(a, 4 * r)
                            for i, c, n, nch in pair:
                                nc.vector.max(top8s[c], cmaxs[c][:, 0:nch]).then_inc(sel, 1)
                            for i, c, n, nch in pair:
                                dve.wait_ge(sel, s0 + 3 + c)
                                ts(nbias[:, i:i + 1], top8s[c][:, 0:1], -SCALE, None, mul)
                                nc.vector.match_replace(marks[c][:, 0:nch], top8s[c], cmaxs[c][:, 0:nch], MARK)\
                                    .then_inc(sel, 1)
                            for i, c, n, nch in pair:
                                mid = n - 2 * P
                                c0 = P // CHUNK
                                dve.wait_ge(sel, s0 + 5 + c)
                                nc.vector.scalar_tensor_tensor(
                                    pens[c][:, 0:mid].rearrange("p (c k) -> p c k", k=CHUNK),
                                    marks[c][:, c0:c0 + mid // CHUNK].unsqueeze(2).broadcast_to([P, mid // CHUNK, CHUNK]),
                                    MARK, old[:, 2 * P - mid:2 * P].rearrange("p (c k) -> p c k", k=CHUNK),
                                    ALU.is_lt, mul).then_inc(sel, 1)
                            for i, c, n, nch in pair:
                                dve.wait_ge(sel, s0 + 7 + c)
                                tt(banks[:, i % 4, P:n - P], banks[:, i % 4, P:n - P], pens[c], add).then_inc(nb_ok, 1)
                                if c == 0:
                                    turned_lo(a, 4 * r + 1)

                        for r in range(4):
                            for i in (4 * r, 4 * r + 1):
                                if i < 2 and not first:
                                    turned_lo(a, i - 2)
                                if i == 0 and not first:
                                    factors(a - 1)
                                largest(i)
                                if i >= 2:
                                    turned_lo(a, i - 2)
                            if r == 3 and not last:
                                queries_lo(j + 1)
                            if r == 1 and not first:
                                scale_output(a - 1)
                            choose(r)
                            if r == 1 and not first:
                                output_lo(j - 1)

                    def turned_lo(a, i):
                        r, t = divmod(i % 16, 4)
                        dve.wait_ge(pt_hi, 16 * a + i + 1)
                        for (dst, src), (hi, _) in zip(turned_tiles(pt_l, r, t, i), turned_tiles(pt_h, r, t, i)):
                            last = tt(dst, src, hi.bitcast(F32), sub)
                        last.then_inc(pt_lo, 1)

                    def factors(a):
                        dve.wait_ge(p_ok, 16 * a + 16)
                        nc.vector.reciprocal(rmax, rsum).then_inc(rinv_s, 1)
                        dve.wait_ge(q_roped, 8 * b + KC)
                        dve.wait_ge(rinv_s, a + 1)
                        nc.vector.tensor_copy(rinvs.rearrange("p (i d) -> p i d", d=HD),
                                              rmax.unsqueeze(2).broadcast_to([P, 16, HD])).then_inc(rinv_ok, 1)
                        dve.wait_ge(rinv_ok, a + 1)

                    def scale_output(a):
                        dve.wait_ge(pv_ok, 4 * a + 4)
                        dve.wait_ge(r_copied, a + 1)
                        tt(rope_b[:], o_bank, rope_a[:], mul).then_inc(o_ok, 1)

                    def output_lo(j):
                        dve.wait_ge(xs_hi, (9 + 2 * b) * KC + 4 * half + j + 1)
                        tt(xs_l[:, 4 * half + j, :], rope_b[:], xs_h[:, 4 * half + j, :].bitcast(F32), sub)\
                            .then_inc(xs_lo, 1)

                    queries_lo(0)
                    four_heads(0, first=True)
                    with dve.Fori(1, 3) as j:
                        four_heads(j)
                    four_heads(3, last=True)
                    turned_lo(8 * b + 4 * half + 4, -2)
                    factors(8 * b + 4 * half + 3)
                    turned_lo(8 * b + 4 * half + 4, -1)
                    scale_output(8 * b + 4 * half + 3)
                    output_lo(3)
                for n in range(12, 20):
                    post(uc + n)
                    xo = x[:, b, n - 12, :]
                    tt(xo, banks[:, n % RING, :], xo, add).then_inc(freed_v, 1)
                    split_unit(uc + n + RING, n)
                    add_chunk(8 + b, b, n - 12, C_FV + b * KC + n - 12 + 1)

            for b in range(NB):
                fill(16 + b, b)
                post(E_U + b)
                split_unit(E_U + b + RING, b)
                if b == 0:
                    ln_centre(11, NB - 1)
                if b == 1:
                    ln_scale(11, NB - 1)
            dve.wait_ge(bm_hi, 1)
            tt(bm_l[:], b_raw[:], bm_h[:].bitcast(F32), sub).then_inc(bm_lo, 1)
            steps = [0]

            def step(instruction):
                steps[0] += 1
                instruction.then_inc(rtv, 1)
                dve.wait_ge(rtv, steps[0])

            def by8(c):
                return rt[:, c:c + 64].rearrange("p (m e) -> p m e", e=NE)

            def each(c):
                return rt[:, c:c + 8].unsqueeze(2).broadcast_to([P, 8, NE])

            dve.wait_ge(rtp, 1)
            step(nc.vector.tensor_copy(by8(0), ln_bank[:, 0:8 * EW].rearrange("p (m e) -> p m e", e=EW)[:, :, RANK:EW]))
            step(nc.vector.tensor_copy(rt[:, 64:128], banks[:, 5, 0:64]))
            step(nc.vector.tensor_reduce(rt[:, 128:129], rt[:, 0:64], AX, ALU.max, apply_absolute_value=True))
            step(nc.vector.tensor_reduce(rt[:, 129:130], rt[:, 64:128], AX, ALU.max, apply_absolute_value=True))
            dve.wait_ge(rtg, 1)
            step(ts(rt[:, 132:134], rt[:, 130:132], 1e-6, None, ALU.max))
            step(nc.vector.reciprocal(rt[:, 134:136], rt[:, 132:134]))
            step(ts(rt[:, 136:138], rt[:, 134:136], 0.5, None, mul))
            step(ts(rt[:, 192:256], rt[:, 64:128], rt[:, 137:138], None, mul))
            step(stt(rt[:, 192:256], rt[:, 0:64], rt[:, 136:137], rt[:, 192:256], mul, add))
            step(nc.vector.tensor_reduce(rt[:, 384:392], by8(192), AX, ALU.max))
            step(tt(by8(256), by8(192), each(384), sub))
            dve.wait_ge(rta, 1)
            step(nc.vector.tensor_reduce(rt[:, 392:400], by8(320), AX, ALU.add))
            step(nc.vector.reciprocal(rt[:, 400:408], rt[:, 392:400]))
            step(tt(by8(448), by8(320), each(400), mul))
            for m in range(8):
                step(nc.vector.max(rt[:, 512 + 8 * m:520 + 8 * m], rt[:, 448 + 8 * m:456 + 8 * m]))
            step(tt(by8(576), by8(448), by8(512)[:, :, 1:2].broadcast_to([P, 8, NE]), sub))
            dve.wait_ge(rta, 2)
            step(ts(rt[:, 704:768], rt[:, 640:704], 1.0, None, add))
            step(nc.vector.reciprocal(rt[:, 640:704], rt[:, 704:768]))
            step(tt(rt[:, 704:768], rt[:, 640:704], rt[:, 448:512], mul))
            step(nc.vector.tensor_reduce(rt[:, 408:416], by8(704), AX, ALU.add))
            step(ts(rt[:, 416:424], rt[:, 408:416], 1e-9, None, add))
            step(nc.vector.reciprocal(rt[:, 424:432], rt[:, 416:424]))
            step(tt(by8(768), by8(704), each(424), mul))
            dve.wait_ge(rtp, 2)
            step(nc.vector.tensor_copy(rt[0:NE, 1024:1536], banks[0:NE, 5, :]))
            step(nc.vector.tensor_copy(rt[0:NE, 1536:2048], banks[0:NE, 7, :]))
            dve.wait_ge(rtp, 3)
            for m, bank in ((0, 4), (1, 6)):
                half = slice(m * 2 * T, (m + 1) * 2 * T)
                step(stt(zp[:, half].rearrange("p (n a) -> p n a", a=2), zh[0:RANK, half].rearrange("p (n a) -> p n a", a=2),
                         0.5, banks[0:RANK, bank, :].unsqueeze(2).broadcast_to([RANK, T, 2]), mul, mul))
            assert steps[0] == MIXED

            def f_block(b, ln, more):
                fill(20 + b, b)
                dve.wait_ge(zs_hi, b + 1)
                tt(zs_l[:], zp[:, bass.ds(b * T, T)], zs_h[:].bitcast(F32), sub).then_inc(zs_lo, 1)
                for n in range(F_N):
                    post(F_U + b * F_N + n)
                    xo = x[:, b, n, :]
                    stt(xo, banks[:, n % RING, :], bias1[:, n:n + 1], xo, add, add).then_inc(freed_v, 1)
                    if more or n < 4:
                        split_unit(F_U + b * F_N + n + RING, n)
                    add_chunk(12 + b, b, n, F_FV + b * KC + n + 1)
                    if ln and n == 1:
                        ln_centre(11 + b, b - 1)
                    if ln and n == 5:
                        ln_scale(11 + b, b - 1)
            f_block(0, False, True)
            with dve.Fori(1, NB - 1) as b:
                f_block(b, True, True)
            f_block(NB - 1, True, False)
            ln_centre(15, NB - 1)
            ln_scale(15, NB - 1)

        @block.tensor
        def _(pe):
            mm = nc.tensor.matmul
            passes = ((w_h, xs_h), (w_h, xs_l), (w_l, xs_h))

            def ln_mean(n):
                pe.wait_ge(summed, (n + 1) * 7)
                if not isinstance(n, int) or n >= 1:
                    pe.wait_ge(normed, n * KC)
                mm(ln_bank, ones[:], full_sum[:], start=True, stop=True).then_inc(mean_ok, 1)

            def ln_var(n):
                pe.wait_ge(sq_added, (n + 1) * 7)
                mm(ln_bank, ones[:], sq_sum[:], start=True, stop=True).then_inc(var_ok, 1)

            def product(u, n, m=P, fill=None, free=False, more=()):
                pe.wait_ge(unit_lo, u + 1)
                for k in range(KC):
                    if fill is not None:
                        pe.wait_ge(xs_lo, fill * KC + k + 1)
                    for c, (w, xs) in enumerate(passes):
                        last = mm(banks[0:m, n % RING, :], w[:, n % RING, k * P:k * P + m], xs[:, k, :],
                                  start=(k == 0 and c == 0), stop=(k == KC - 1 and c == 2 and not more))
                    if free and k < KC - 1:
                        last.then_inc(xs_free, 1)
                for c, (w, z) in enumerate(more):
                    last = mm(banks[0:m, n % RING, :], w, z, start=False, stop=(c == len(more) - 1))
                last.then_inc(unit_done, 1)

            pe.wait_ge(consts_in, 160)

            def a_block(b, ln):
                for n in range(A_N):
                    if not isinstance(b, int) or n >= RING:
                        pe.wait_ge(freed_v, b * A_N + n - RING + 1)
                    product(A_U + b * A_N + n, n, fill=b if n == 0 else None, free=n == A_N - 1)
                    if ln and n == 1:
                        ln_mean(b - 1)
                    if ln and n == 5:
                        ln_var(b - 1)
            a_block(0, False)
            with pe.Fori(1, NB) as b:
                a_block(b, True)

            def gate_up(u0, h0, freed, fill=None, norm=None):
                for n in range(2 * G):
                    if n < RING:
                        pe.wait_ge(freed_v, freed - RING + n + 1)
                        if norm is None:
                            pe.wait_ge(h_ok, h0 - RING // 2 + n // 2 + 1)
                    else:
                        pe.wait_ge(h_ok, h0 + (n - RING) // 2 + 1)
                    product(u0 + n, n, fill=fill if n == 0 else None)
                    if norm is not None and n == 1:
                        ln_mean(norm)
                    if norm is not None and n == 5:
                        ln_var(norm)

            def down(u0, h0, buf, freed, h_before=None):
                pe.wait_ge(h_lo, h0 + G)
                for q in range(4):
                    pe.wait_ge(unit_lo, u0 + q + 1)
                    for oo in range(2):
                        o = 2 * q + oo
                        if o < RING and h_before is not None:
                            pe.wait_ge(h_ok, h_before + G - RING // 2 + o // 2 + 1)
                        else:
                            pe.wait_ge(freed_v, freed - RING + o + 1)
                        for i in range(G):
                            w0 = (oo * G + i) * P
                            for c, (w, hs) in enumerate(((w_h, hs_h), (w_h, hs_l), (w_l, hs_h))):
                                last = mm(banks[:, o % RING, :], w[:, q, w0:w0 + P], hs[:, buf, i, :],
                                          start=(i == 0 and c == 0), stop=(i == G - 1 and c == 2))
                    last.then_inc(unit_done, 1)

            with pe.Fori(0, NB) as b:
                ub, hb, fv = B_U + b * B_N, b * NG * G, B_FV + b * B_FREED
                gate_up(ub, hb, fv, fill=4 + b, norm=3 + b)
                with pe.Fori(0, NG // 2) as j:
                    gate_up(ub + 8 + j * 24, hb + 4 + j * 8, fv + j * 16)
                    down(ub + 16 + j * 24, hb + j * 8, 0, fv + j * 16, h_before=hb + 4 + j * 8)
                    gate_up(ub + 20 + j * 24, hb + 8 + j * 8, fv + j * 16 + 8)
                    down(ub + 28 + j * 24, hb + 4 + j * 8, 1, fv + j * 16 + 8, h_before=hb + 8 + j * 8)
                down(ub + 80, hb + 24, 0, fv + 48)

            pe.wait_ge(rope_in, 32)
            with pe.Fori(0, NB) as b:
                uc = C_U + b * C_N
                for n in range(12):
                    if n < RING:
                        pe.wait_ge(freed_v, C_FV + b * KC + n - RING + 1)
                    else:
                        pe.wait_ge(freed_a, b * C_FA + n - RING + 1)
                    if n not in (2, 3):
                        product(uc + n, n, fill=8 + 2 * b if n == 0 else None)
                    elif n == 3:
                        pe.wait_ge(unit_lo, uc + 4)
                        for t in range(QT):
                            dst = banks[:, 2 + t // 2, t % 2 * 2 * P:(t % 2 + 1) * 2 * P]
                            for k in range(KC):
                                for c, (w, xs) in enumerate(passes):
                                    last = mm(dst, xs[:, k, t * P:(t + 1) * P], w[:, 2:4, k * P:(k + 1) * P],
                                              start=(k == 0 and c == 0), stop=(k == KC - 1 and c == 2))
                        last.then_inc(unit_done, 2)
                    if n == 3:
                        ln_mean(7 + b)
                    if n == 9:
                        ln_var(7 + b)
                for half in range(2):
                    def scores(a, i):
                        r, t = divmod(i, 4)
                        n = P * (t + 1)
                        q_at, rows = slice(t * P, n), slice(HD * r, HD * r + HD)
                        for c, (q, k) in enumerate(((qs_h, kt_h), (qs_h, kt_l), (qs_l, kt_h))):
                            mm(banks[:, i % 4, 0:n], q[rows, q_at], k[rows, half, 0:n], start=c == 0, stop=False)
                        mm(banks[:, i % 4, t * P:n], ident_b[:], causal_b[:], start=False, stop=True)\
                            .then_inc(scored, 1)

                    def turn(a, i):
                        for u, kt in enumerate(TURN_ORDER[i % 4]):
                            last = nc.tensor.transpose(t_bank[i % 2][:, u * P:(u + 1) * P],
                                                       prob[:, i % 2, kt * P:(kt + 1) * P], ident[:])
                        last.then_inc(turned, 1)

                    def values(r):
                        for kt in range(QT):
                            n = T - kt * P
                            for c, (v, p) in enumerate(((vp_h, pt_h), (vp_h, pt_l), (vp_l, pt_h))):
                                last = mm(o_bank[:, kt * P:T], v[:, kt, V_WIN[r]:V_WIN[r] + P],
                                          p[:, r % 2, PT_AT[kt] * P:PT_AT[kt] * P + n],
                                          start=(r == 0 and kt == 0 and c == 0), stop=(r == 3 and kt == 3 and c == 2))
                        last.then_inc(pv_ok, 1)

                    def factors(a):
                        pe.wait_ge(rinv_ok, a + 1)
                        for t in range(QT):
                            last = nc.tensor.transpose(ln_bank[:, t * P:(t + 1) * P], rinvs[:, t * P:(t + 1) * P],
                                                       ident[:])
                        last.then_inc(rinv_t, 1)

                    def four_heads(j, first=False, last=False):
                        a = 8 * b + 4 * half + j
                        for i in range(16):
                            pe.wait_ge(p_ok, 16 * a + i + 1)
                            if i >= 2 or not first:
                                pe.wait_ge(pt_lo, 16 * a + i - 1)
                            turn(a, i)
                            if i + 3 < 16:
                                if i + 3 >= 4 or not first:
                                    pe.wait_ge(p_ok, 16 * a + i)
                                scores(a, i + 3)
                            elif not last:
                                pe.wait_ge(q_lo, 8 * b + 4 * half + j + 2)
                                scores(a + 1, i - 13)
                            r = (i - 5) // 4
                            if i % 4 == 1 and (r >= 0 or not first):
                                pe.wait_ge(pt_lo, 16 * a + 4 * r + 4)
                                if i == 5 and not first:
                                    pe.wait_ge(o_ok, a)
                                values(r % 4)
                            if i == 2 and not first:
                                factors(a - 1)

                    a0 = 8 * b + 4 * half
                    pe.wait_ge(freed_a, (b + 1) * C_FA)
                    pe.wait_ge(normed, (8 + b) * KC)
                    pe.wait_ge(vp_lo, a0 + 4)
                    pe.wait_ge(roped_lo, 2 * b + 2)
                    pe.wait_ge(q_lo, a0 + 1)
                    for i in range(3):
                        scores(a0, i)
                    four_heads(0, first=True)
                    with pe.Fori(1, 3) as j:
                        four_heads(j)
                    four_heads(3, last=True)
                    pe.wait_ge(pt_lo, 16 * a0 + 64)
                    values(3)
                    factors(a0 + 3)
                for n in range(12, 20):
                    if n >= 16:
                        pe.wait_ge(freed_v, C_FV + b * KC + n - 16 + 1)
                    product(uc + n, n, fill=9 + 2 * b if n == 12 else None)

            for b in range(NB):
                pe.wait_ge(freed_v, F_FV - RING + b + 1)
                product(E_U + b, b, fill=16 + b)
                if b == 0:
                    ln_mean(11)
                if b == 1:
                    ln_var(11)
            pe.wait_ge(late_in, 48)
            pe.wait_ge(freed_a, NB * C_FA + NB)
            pe.wait_ge(normed, 12 * KC)
            for m in range(8):
                last_of_pair = zh[:, m * 2 * P:(m + 1) * 2 * P].rearrange("p (n a) -> p n a", a=2)[:, :, 1]
                nc.tensor.transpose(ln_bank[:, m * EW:(m + 1) * EW], last_of_pair[0:EW, :], ident[0:EW, 0:EW])
            for m in range(8):
                last_of_pair = zh[:, m * 2 * P:(m + 1) * 2 * P].rearrange("p (n a) -> p n a", a=2)[:, :, 1]
                last = mm(banks[:, 5, m * NE:(m + 1) * NE], last_of_pair[0:RANK, :], li_t[:], start=True, stop=True)
            last.then_inc(rtp, 1)
            pe.wait_ge(rtv, WEIGHED)
            for m in range(8):
                last = nc.tensor.transpose(banks[0:NE, 5 + m // 4 * 2, m % 4 * P:(m % 4 + 1) * P],
                                           rt[:, 768 + m * NE:768 + (m + 1) * NE], ident[:])
            last.then_inc(rtp, 1)
            pe.wait_ge(rtv, TURNED_W)
            mm(banks[0:RANK, 4, :], li[:], rt[0:NE, 1024:1536], start=True, stop=True)
            mm(banks[0:RANK, 6, :], li[:], rt[0:NE, 1536:2048], start=True, stop=True).then_inc(rtp, 1)
            pe.wait_ge(bm_lo, 1)
            pe.wait_ge(rtv, MIXED)

            def f_block(b, ln):
                for n in range(F_N):
                    pe.wait_ge(freed_v, F_FV + b * F_N + n - RING + 1)
                    if n == 0:
                        pe.wait_ge(zs_lo, b + 1)
                    o = slice(n * P, (n + 1) * P)
                    product(F_U + b * F_N + n, n, fill=20 + b if n == 0 else None,
                            more=((bm_h[:, o], zs_h[:]), (bm_h[:, o], zs_l[:]), (bm_l[:, o], zs_h[:])))
                    if ln and n == 1:
                        ln_mean(11 + b)
                    if ln and n == 5:
                        ln_var(11 + b)
            f_block(0, False)
            with pe.Fori(1, NB) as b:
                f_block(b, True)
            ln_mean(15)
            ln_var(15)


def unit_of(w):
    return w.reshape(-1, P, w.shape[1] // P, P).transpose(0, 3, 2, 1).reshape(-1, P, w.shape[1])


def layout(i):
    f32 = np.float32
    units = [unit_of(i["L0_attn_weight"])]
    gate, up = unit_of(i["L0_ffn_gate_w"]), unit_of(i["L0_ffn_up_w"])
    dn = i["L0_ffn_down_w"].reshape(4, 2, P, NG, G, P).transpose(3, 0, 5, 1, 4, 2).reshape(NG, 4, P, D)

    def gu(g):
        return np.stack([gate[g * G:(g + 1) * G], up[g * G:(g + 1) * G]], 1).reshape(2 * G, P, D)
    units.append(gu(0))
    for g in range(1, NG):
        units += [gu(g), dn[g - 1]]
    units.append(dn[NG - 1])
    wq = i["L1_attn_wq"].reshape(2, 4, 4, HD, D).transpose(0, 2, 1, 3, 4).reshape(D, D)
    wo = i["L1_attn_wo"].reshape(D, 2, 4, 4, HD).transpose(0, 1, 3, 2, 4).reshape(D, D)
    units += [unit_of(i["L1_attn_wk"]), unit_of(i["L1_attn_wv"]), unit_of(wq), unit_of(wo)]
    e = np.zeros((1, P, KC, P), f32)
    e[0, :, :, 0:RANK] = i["L1_ffn_A"].reshape(KC, P, RANK).transpose(1, 0, 2)
    e[0, :, :, RANK:EW] = i["L1_ffn_W"][0:NE].reshape(NE, KC, P).transpose(2, 1, 0)
    units += [e.reshape(1, P, D), unit_of(i["L1_ffn_W"])]
    units = np.concatenate(units)
    assert units.shape == (N_UNITS, P, D)

    inv = (1.0 / f32(10000.0) ** (np.arange(0, HD, 2, dtype=f32) / f32(HD))).astype(f32)
    angle = np.arange(T, dtype=f32)[:, None] * inv[None, :]
    cos, sin = np.cos(angle).astype(f32).T, np.sin(angle).astype(f32).T
    sin = np.concatenate([-sin, sin])
    q, k = np.arange(P)[:, None], np.arange(P)[None, :]
    bias_e = np.zeros((P, 1), f32)
    bias_e[RANK:EW, 0] = i["L1_ffn_b"][0:NE]
    bf = mybir.dt.np(BF16)
    return {
        "units": units,
        "x": np.ascontiguousarray(i["L0_attn_x"].reshape(NB, T, KC, P).transpose(0, 3, 2, 1)),
        "ones": np.full((P, P), 1.0 / D, f32),
        "ident": np.eye(P, dtype=f32),
        "ident_b": np.eye(P).astype(bf),
        "causal_b": np.where(k > q, NEG, 0.0).astype(bf),
        "old": np.concatenate([np.full((P, P), NEG, f32), np.where(k > q, 0.0, NEG).astype(f32)], 1),
        "bias0": np.ascontiguousarray(i["L0_attn_bias"].reshape(KC, P).T),
        "lnw": np.ascontiguousarray(i["L0_ffn_ln_w"].reshape(KC, P).T),
        "bias1": np.ascontiguousarray(i["L1_ffn_b"].reshape(KC, P).T),
        "bias_e": bias_e,
        "eps": np.full((P, 1), LN_EPS, f32),
        "cos": np.tile(np.concatenate([cos, cos]), (4, 1)),
        "sin": np.tile(sin, (4, 1)),
        "bmat": i["L1_ffn_Bmat"],
        "li": i["L1_ffn_LiMEs"],
        "li_t": np.ascontiguousarray(i["L1_ffn_LiMEs"].T),
    }


def kernel(**inputs):
    import concourse.bacc as bacc
    from concourse.bass_utils import run_bass_kernel_spmd

    arrays = layout({name: np.asarray(a) for name, a in inputs.items()})
    nc = bacc.Bacc("TRN2", target_bir_lowering=False, num_devices=1, dynamic_dma_scratch_size=SCRATCH)
    io = {name: nc.dram_tensor(f"in_{name}", a.shape, mybir.dt.from_np(a.dtype), kind="ExternalInput").ap()
          for name, a in arrays.items()}
    io["out"] = nc.dram_tensor("out_x", (NB, P, KC, T), F32, kind="ExternalOutput").ap()
    build(nc, io)
    r = run_bass_kernel_spmd(nc, [{f"in_{name}": a for name, a in arrays.items()}], core_ids=[0])
    return r.results[0]["out_x"].transpose(0, 3, 2, 1).reshape(NB, T, D)
```
